# Optimizing a Trainium2 kernel written in Bass

```python
import numpy as np
import jax
import jax.numpy as jnp

def _softmax(x, axis=-1):
    return jax.nn.softmax(x, axis=axis)

def _gelu(x):
    return jax.nn.gelu(x, approximate=True)

def _silu(x):
    return jax.nn.silu(x)

def _sigmoid(x):
    return jax.nn.sigmoid(x)

def _layernorm(x, axis=-1, eps=1e-05):
    m = jnp.mean(x, axis=axis, keepdims=True)
    v = jnp.var(x, axis=axis, keepdims=True)
    return (x - m) / jnp.sqrt(v + eps)

def _scatter_add(tgt, idx, src, axis=0):
    return tgt.at[idx].add(src)

def _segment_sum(src, seg, n):
    return jax.ops.segment_sum(src, seg, n)
kernel_name = 'mk_lm_tower_d1_tok_ids512_r4_1aec15'

def setup_inputs(seed: int=0):
    np.random.seed(seed)
    _w = jnp.asarray

    def _rec_inputs():
        import jax
        import jax.numpy as jnp
        _rk = jax.random.key(seed)
        x = jax.random.randint(jax.random.fold_in(_rk, 1), (8, 256), 0, 2, jnp.int32)
        fside_BSS_pre_trace = jax.random.uniform(jax.random.fold_in(_rk, 21), (8, 256, 256), jnp.float32, 0.0, 0.1)
        fside_BSS_post_trace = jax.random.uniform(jax.random.fold_in(_rk, 22), (8, 256, 256), jnp.float32, 0.0, 0.1)
        fside_BSS_attention = jax.random.uniform(jax.random.fold_in(_rk, 23), (8, 256, 256), jnp.float32, 0.0, 1)
        return (x, fside_BSS_pre_trace, fside_BSS_post_trace, fside_BSS_attention)
    x, fside_BSS_pre_trace, fside_BSS_post_trace, fside_BSS_attention = _rec_inputs()

    def _L0_tok_setup():
        import jax, jax.numpy as jnp
        import numpy as np
        MIN_ATTN = -0.5
        MAX_ATTN = 1.5
        DT = 0.001
        B, N, E = (8, 256, 128)
        key = jax.random.key(seed)
        ks = jax.random.split(key, 10)
        spikes = jax.random.randint(ks[0], (B, N), 0, 2, dtype=jnp.int32)
        pre_trace = jax.random.uniform(ks[1], (B, N, N), dtype=jnp.float32) * 0.1
        post_trace = jax.random.uniform(ks[2], (B, N, N), dtype=jnp.float32) * 0.1
        attention = jax.random.uniform(ks[3], (B, N, N), dtype=jnp.float32)
        std = np.sqrt(1.0 / N).astype(np.float32)
        latent_pre_weight = jax.random.normal(ks[4], (1, N, N), dtype=jnp.float32) * std
        latent_post_weight = jax.random.normal(ks[5], (1, N, N), dtype=jnp.float32) * std
        latent_pre_tau_s = jnp.zeros((1, N, N), dtype=jnp.float32)
        latent_post_tau_s = jnp.zeros((1, N, N), dtype=jnp.float32)
        v_w = jax.random.normal(ks[6], (E, N), dtype=jnp.float32) * std
        v_b = jax.random.normal(ks[7], (E,), dtype=jnp.float32) * 0.01
        return {'spikes': spikes, 'pre_trace': pre_trace, 'post_trace': post_trace, 'attention': attention, 'latent_pre_weight': latent_pre_weight, 'latent_post_weight': latent_post_weight, 'latent_pre_tau_s': latent_pre_tau_s, 'latent_post_tau_s': latent_post_tau_s, 'v_w': v_w, 'v_b': v_b}
    _L0_tok_all = _L0_tok_setup()
    _L0_tok_in = {k: v for k, v in _L0_tok_all.items() if k in ('latent_pre_weight', 'latent_post_weight', 'latent_pre_tau_s', 'latent_post_tau_s', 'v_w', 'v_b')}
    del _L0_tok_all

    def _L0_attn_setup():
        import jax, jax.numpy as jnp
        import numpy as np
        N_HEAD = 8
        D_MODEL = 128
        D_HEAD = 64
        N_ROLL = 2
        SLEN = 512
        BSZ = 8
        EPS = 1e-05
        SCALE = D_HEAD ** (-0.5)

        def _dpfp(x):
            x = jnp.concatenate([jax.nn.relu(x), jax.nn.relu(-x)], axis=-1)
            x = jnp.concatenate([x * jnp.roll(x, i, axis=-1) for i in range(1, N_ROLL + 1)], axis=-1)
            return x / x.sum(-1, keepdims=True)
        key = jax.random.key(seed)
        k1, k2, k3 = jax.random.split(key, 3)
        h = jax.random.normal(k1, (SLEN, BSZ, D_MODEL), dtype=jnp.float32)
        W_qkvb = jax.random.normal(k2, (N_HEAD * (3 * D_HEAD + 1), D_MODEL), dtype=jnp.float32) * 0.02
        W_o = jax.random.normal(k3, (D_MODEL, N_HEAD * D_HEAD), dtype=jnp.float32) * 0.02
        ln_g = jnp.ones((D_MODEL,), dtype=jnp.float32)
        ln_b = jnp.zeros((D_MODEL,), dtype=jnp.float32)
        return {'h': h, 'W_qkvb': W_qkvb, 'W_o': W_o, 'ln_g': ln_g, 'ln_b': ln_b}
    _L0_attn_all = _L0_attn_setup()
    _L0_attn_in = {k: v for k, v in _L0_attn_all.items() if k in ('W_qkvb', 'W_o', 'ln_g', 'ln_b')}
    del _L0_attn_all

    def _L0_ffn_setup():
        import jax, jax.numpy as jnp
        import numpy as np
        MARK_AX = 0
        OP_AND = 1
        OP_OR = 2
        OP_XOR = 3
        ALU_LO = 16
        ALU_HI = 32
        AX_CARRY_LO = 48
        AX_CARRY_HI = 64
        OUTPUT_LO = 80
        OUTPUT_HI = 96
        NIB_A = 0
        NIB_B = 1
        OP_START = 16
        RESULT = 64
        GE_DIM = 160
        N_ROWS = 8
        B, S, D = (8, 1024, 128)

        def _decode_nibble(x_bd, start):
            bits = x_bd[..., start:start + 16] > 0.5
            return jnp.argmax(bits, axis=-1).astype(x_bd.dtype)

        def _mlp2(x, w1, b1, w2, b2):
            h = jax.nn.relu(jnp.einsum('bsrd,de->bsre', x, w1) + b1)
            return jnp.einsum('bsrd,de->bsre', h, w2) + b2

        def _forward(x_bd, and_w1, and_b1, and_w2, and_b2, or_w1, or_b1, or_w2, or_b2, xor_w1, xor_b1, xor_w2, xor_b2):
            a_lo = _decode_nibble(x_bd, ALU_LO)
            a_hi = _decode_nibble(x_bd, ALU_HI)
            b_lo = _decode_nibble(x_bd, AX_CARRY_LO)
            b_hi = _decode_nibble(x_bd, AX_CARRY_HI)
            Bsz, Ssz, _ = x_bd.shape
            x_ge = jnp.zeros((Bsz, Ssz, N_ROWS, GE_DIM), x_bd.dtype)
            x_ge = x_ge.at[..., 0, NIB_A].set(a_lo).at[..., 1, NIB_A].set(a_hi)
            x_ge = x_ge.at[..., 0, NIB_B].set(b_lo).at[..., 1, NIB_B].set(b_hi)
            x_ge = x_ge.at[..., :, OP_START + 28].set(x_bd[..., OP_OR, None])
            x_ge = x_ge.at[..., :, OP_START + 29].set(x_bd[..., OP_XOR, None])
            x_ge = x_ge.at[..., :, OP_START + 30].set(x_bd[..., OP_AND, None])
            y_and = _mlp2(x_ge, and_w1, and_b1, and_w2, and_b2)
            y_or = _mlp2(x_ge, or_w1, or_b1, or_w2, or_b2)
            y_xor = _mlp2(x_ge, xor_w1, xor_b1, xor_w2, xor_b2)
            is_and = x_bd[..., OP_AND] > 0.5
            is_or = x_bd[..., OP_OR] > 0.5
            is_xor = x_bd[..., OP_XOR] > 0.5
            sel = jnp.where(is_and[..., None, None], y_and, jnp.where(is_or[..., None, None], y_or, y_xor))
            active = (x_bd[..., MARK_AX] >= 0.5) & (is_and | is_or | is_xor)
            res_lo = jnp.clip(jnp.round(sel[..., 0, RESULT]), 0, 15).astype(jnp.int32)
            res_hi = jnp.clip(jnp.round(sel[..., 1, RESULT]), 0, 15).astype(jnp.int32)
            amask = active.astype(x_bd.dtype)[..., None]
            add_lo = 2.0 * jax.nn.one_hot(res_lo, 16, dtype=x_bd.dtype) * amask
            add_hi = 2.0 * jax.nn.one_hot(res_hi, 16, dtype=x_bd.dtype) * amask
            out = x_bd.at[..., OUTPUT_LO:OUTPUT_LO + 16].add(add_lo)
            out = out.at[..., OUTPUT_HI:OUTPUT_HI + 16].add(add_hi)
            return out
        key = jax.random.key(seed)
        ks = jax.random.split(key, 7)
        inp = {'x_bd': jax.random.uniform(ks[0], (B, S, D), dtype=jnp.float32)}
        for i, op in enumerate(['and', 'or', 'xor']):
            inp[op + '_w1'] = jax.random.normal(ks[1 + 2 * i], (GE_DIM, GE_DIM), jnp.float32) * 0.08
            inp[op + '_b1'] = jnp.zeros((GE_DIM,), jnp.float32)
            inp[op + '_w2'] = jax.random.normal(ks[2 + 2 * i], (GE_DIM, GE_DIM), jnp.float32) * 0.08
            inp[op + '_b2'] = jnp.zeros((GE_DIM,), jnp.float32)
        return inp
    _L0_ffn_all = _L0_ffn_setup()
    _L0_ffn_in = {k: v for k, v in _L0_ffn_all.items() if k in ('and_w1', 'and_b1', 'and_w2', 'and_b2', 'or_w1', 'or_b1', 'or_w2', 'or_b2', 'xor_w1', 'xor_b1', 'xor_w2', 'xor_b2')}
    del _L0_ffn_all
    return {'x': x, 'fside_BSS_pre_trace': fside_BSS_pre_trace, 'fside_BSS_post_trace': fside_BSS_post_trace, 'fside_BSS_attention': fside_BSS_attention, 'L0_tok_latent_pre_weight': _L0_tok_in['latent_pre_weight'], 'L0_tok_latent_post_weight': _L0_tok_in['latent_post_weight'], 'L0_tok_latent_pre_tau_s': _L0_tok_in['latent_pre_tau_s'], 'L0_tok_latent_post_tau_s': _L0_tok_in['latent_post_tau_s'], 'L0_tok_v_w': _L0_tok_in['v_w'], 'L0_tok_v_b': _L0_tok_in['v_b'], 'L0_attn_W_qkvb': _L0_attn_in['W_qkvb'], 'L0_attn_W_o': _L0_attn_in['W_o'], 'L0_attn_ln_g': _L0_attn_in['ln_g'], 'L0_attn_ln_b': _L0_attn_in['ln_b'], 'L0_ffn_and_w1': _L0_ffn_in['and_w1'], 'L0_ffn_and_b1': _L0_ffn_in['and_b1'], 'L0_ffn_and_w2': _L0_ffn_in['and_w2'], 'L0_ffn_and_b2': _L0_ffn_in['and_b2'], 'L0_ffn_or_w1': _L0_ffn_in['or_w1'], 'L0_ffn_or_b1': _L0_ffn_in['or_b1'], 'L0_ffn_or_w2': _L0_ffn_in['or_w2'], 'L0_ffn_or_b2': _L0_ffn_in['or_b2'], 'L0_ffn_xor_w1': _L0_ffn_in['xor_w1'], 'L0_ffn_xor_b1': _L0_ffn_in['xor_b1'], 'L0_ffn_xor_w2': _L0_ffn_in['xor_w2'], 'L0_ffn_xor_b2': _L0_ffn_in['xor_b2']}

def reference(x, fside_BSS_pre_trace, fside_BSS_post_trace, fside_BSS_attention, L0_tok_latent_pre_weight, L0_tok_latent_post_weight, L0_tok_latent_pre_tau_s, L0_tok_latent_post_tau_s, L0_tok_v_w, L0_tok_v_b, L0_attn_W_qkvb, L0_attn_W_o, L0_attn_ln_g, L0_attn_ln_b, L0_ffn_and_w1, L0_ffn_and_b1, L0_ffn_and_w2, L0_ffn_and_b2, L0_ffn_or_w1, L0_ffn_or_b1, L0_ffn_or_w2, L0_ffn_or_b2, L0_ffn_xor_w1, L0_ffn_xor_b1, L0_ffn_xor_w2, L0_ffn_xor_b2):
    import jax
    import jax.numpy as jnp

    def _L0_tok_ref(spikes, pre_trace, post_trace, attention, latent_pre_weight, latent_post_weight, latent_pre_tau_s, latent_post_tau_s, v_w, v_b):
        import jax, jax.numpy as jnp
        import numpy as np
        MIN_ATTN = -0.5
        MAX_ATTN = 1.5
        DT = 0.001
        B, N, E = (8, 256, 128)
        s = spikes.astype(jnp.float32)
        pre_spikes = s[:, None, :]
        post_spikes = s[:, :, None]
        pre_decay = jnp.exp(-DT / jnp.exp(latent_pre_tau_s))
        post_decay = jnp.exp(-DT / jnp.exp(latent_post_tau_s))
        pre_trace = pre_trace * pre_decay + pre_spikes * jnp.exp(latent_pre_weight) * DT
        post_trace = post_trace * post_decay + post_spikes * jnp.exp(latent_post_weight) * DT
        post_mask = (post_spikes != 0).astype(jnp.float32)
        pre_mask = (pre_spikes != 0).astype(jnp.float32)
        attention = jnp.clip(attention + (1.0 - attention) * (pre_trace * post_mask) - attention * (post_trace * pre_mask), MIN_ATTN, MAX_ATTN)
        out = jnp.einsum('bij,ej->bie', attention, v_w) + v_b
        return out

    def _L0_attn_ref(h, W_qkvb, W_o, ln_g, ln_b):
        import jax, jax.numpy as jnp
        import numpy as np
        N_HEAD = 8
        D_MODEL = 128
        D_HEAD = 64
        N_ROLL = 2
        SLEN = 512
        BSZ = 8
        EPS = 1e-05
        SCALE = D_HEAD ** (-0.5)

        def _dpfp(x):
            x = jnp.concatenate([jax.nn.relu(x), jax.nn.relu(-x)], axis=-1)
            x = jnp.concatenate([x * jnp.roll(x, i, axis=-1) for i in range(1, N_ROLL + 1)], axis=-1)
            return x / x.sum(-1, keepdims=True)
        slen, bsz, _ = h.shape
        qkvb = jnp.einsum('lbd,ed->lbe', h, W_qkvb).reshape(slen, bsz, N_HEAD, 3 * D_HEAD + 1)
        q, k, v, beta = jnp.split(qkvb, [D_HEAD, 2 * D_HEAD, 3 * D_HEAD], axis=-1)
        beta = jax.nn.sigmoid(beta)
        q = _dpfp(q)
        k = _dpfp(k)
        denom_acc = jnp.cumsum(k, axis=0)
        denominator = jnp.einsum('lbhd,lbhd->lbh', denom_acc, q)[..., None]
        dk = 2 * N_ROLL * D_HEAD
        W0 = jnp.zeros((bsz, N_HEAD, dk, D_HEAD), dtype=h.dtype)

        def step(W, inp):
            qt, kt, vt, bt = inp
            v_old = jnp.einsum('bhd,bhde->bhe', kt, W)
            delta = bt * (vt - v_old)
            W = W + jnp.einsum('bhd,bhe->bhde', kt, delta)
            out = jnp.einsum('bhd,bhde->bhe', qt, W)
            return (W, out)
        _, out = jax.lax.scan(step, W0, (q, k, v, beta))
        out = SCALE * out / (denominator + EPS)
        out = out.reshape(slen, bsz, N_HEAD * D_HEAD)
        attn_out = jnp.einsum('lbe,de->lbd', out, W_o)
        x = h + attn_out
        mu = x.mean(-1, keepdims=True)
        var = x.var(-1, keepdims=True)
        return (x - mu) * jax.lax.rsqrt(var + EPS) * ln_g + ln_b

    def _L0_ffn_ref(x_bd, and_w1, and_b1, and_w2, and_b2, or_w1, or_b1, or_w2, or_b2, xor_w1, xor_b1, xor_w2, xor_b2):
        import jax, jax.numpy as jnp
        import numpy as np
        MARK_AX = 0
        OP_AND = 1
        OP_OR = 2
        OP_XOR = 3
        ALU_LO = 16
        ALU_HI = 32
        AX_CARRY_LO = 48
        AX_CARRY_HI = 64
        OUTPUT_LO = 80
        OUTPUT_HI = 96
        NIB_A = 0
        NIB_B = 1
        OP_START = 16
        RESULT = 64
        GE_DIM = 160
        N_ROWS = 8
        B, S, D = (8, 1024, 128)

        def _decode_nibble(x_bd, start):
            bits = x_bd[..., start:start + 16] > 0.5
            return jnp.argmax(bits, axis=-1).astype(x_bd.dtype)

        def _mlp2(x, w1, b1, w2, b2):
            h = jax.nn.relu(jnp.einsum('bsrd,de->bsre', x, w1) + b1)
            return jnp.einsum('bsrd,de->bsre', h, w2) + b2

        def _forward(x_bd, and_w1, and_b1, and_w2, and_b2, or_w1, or_b1, or_w2, or_b2, xor_w1, xor_b1, xor_w2, xor_b2):
            a_lo = _decode_nibble(x_bd, ALU_LO)
            a_hi = _decode_nibble(x_bd, ALU_HI)
            b_lo = _decode_nibble(x_bd, AX_CARRY_LO)
            b_hi = _decode_nibble(x_bd, AX_CARRY_HI)
            Bsz, Ssz, _ = x_bd.shape
            x_ge = jnp.zeros((Bsz, Ssz, N_ROWS, GE_DIM), x_bd.dtype)
            x_ge = x_ge.at[..., 0, NIB_A].set(a_lo).at[..., 1, NIB_A].set(a_hi)
            x_ge = x_ge.at[..., 0, NIB_B].set(b_lo).at[..., 1, NIB_B].set(b_hi)
            x_ge = x_ge.at[..., :, OP_START + 28].set(x_bd[..., OP_OR, None])
            x_ge = x_ge.at[..., :, OP_START + 29].set(x_bd[..., OP_XOR, None])
            x_ge = x_ge.at[..., :, OP_START + 30].set(x_bd[..., OP_AND, None])
            y_and = _mlp2(x_ge, and_w1, and_b1, and_w2, and_b2)
            y_or = _mlp2(x_ge, or_w1, or_b1, or_w2, or_b2)
            y_xor = _mlp2(x_ge, xor_w1, xor_b1, xor_w2, xor_b2)
            is_and = x_bd[..., OP_AND] > 0.5
            is_or = x_bd[..., OP_OR] > 0.5
            is_xor = x_bd[..., OP_XOR] > 0.5
            sel = jnp.where(is_and[..., None, None], y_and, jnp.where(is_or[..., None, None], y_or, y_xor))
            active = (x_bd[..., MARK_AX] >= 0.5) & (is_and | is_or | is_xor)
            res_lo = jnp.clip(jnp.round(sel[..., 0, RESULT]), 0, 15).astype(jnp.int32)
            res_hi = jnp.clip(jnp.round(sel[..., 1, RESULT]), 0, 15).astype(jnp.int32)
            amask = active.astype(x_bd.dtype)[..., None]
            add_lo = 2.0 * jax.nn.one_hot(res_lo, 16, dtype=x_bd.dtype) * amask
            add_hi = 2.0 * jax.nn.one_hot(res_hi, 16, dtype=x_bd.dtype) * amask
            out = x_bd.at[..., OUTPUT_LO:OUTPUT_LO + 16].add(add_lo)
            out = out.at[..., OUTPUT_HI:OUTPUT_HI + 16].add(add_hi)
            return out
        return _forward(x_bd, and_w1, and_b1, and_w2, and_b2, or_w1, or_b1, or_w2, or_b2, xor_w1, xor_b1, xor_w2, xor_b2)
    h = _L0_tok_ref(x, fside_BSS_pre_trace, fside_BSS_post_trace, fside_BSS_attention, L0_tok_latent_pre_weight, L0_tok_latent_post_weight, L0_tok_latent_pre_tau_s, L0_tok_latent_post_tau_s, L0_tok_v_w, L0_tok_v_b)
    h = h + _L0_attn_ref(_layernorm(h, axis=-1), L0_attn_W_qkvb, L0_attn_W_o, L0_attn_ln_g, L0_attn_ln_b)
    h = h + _L0_ffn_ref(_layernorm(h, axis=-1), L0_ffn_and_w1, L0_ffn_and_b1, L0_ffn_and_w2, L0_ffn_and_b2, L0_ffn_or_w1, L0_ffn_or_b1, L0_ffn_or_w2, L0_ffn_or_b2, L0_ffn_xor_w1, L0_ffn_xor_b1, L0_ffn_xor_w2, L0_ffn_xor_b2)
    return h

_drawn_inputs = setup_inputs


def setup_inputs(seed=0):
    import zlib

    import numpy as np

    out = dict(_drawn_inputs(seed))
    spreads = {'L0_tok_latent_pre_tau_s': (0.0, 2.0),
     'L0_tok_latent_post_tau_s': (0.0, 2.0),
     'L0_attn_ln_g': (1.0, 0.2),
     'L0_attn_ln_b': (0.0, 0.1),
     'L0_ffn_and_b1': (0.0, 0.1),
     'L0_ffn_and_b2': (0.0, 0.1),
     'L0_ffn_or_b1': (0.0, 0.8),
     'L0_ffn_or_b2': (0.0, 0.558),
     'L0_ffn_xor_b1': (0.0, 0.1),
     'L0_ffn_xor_b2': (0.0, 0.1)}
    factors = {'L0_tok_latent_pre_weight': 64.0,
     'L0_tok_latent_post_weight': 64.0,
     'L0_attn_W_qkvb': 7.666,
     'L0_attn_W_o': 8.0,
     'L0_ffn_or_w2': 2.867}
    for name, (base, spread) in spreads.items():
        noise = np.random.default_rng([zlib.crc32(name.encode()), seed]).standard_normal(out[name].shape)
        drawn = base * np.exp(spread * noise) if base else spread * noise
        out[name] = jnp.asarray(drawn.astype(out[name].dtype))
    for name, factor in factors.items():
        out[name] = (out[name] * factor).astype(out[name].dtype)
    return out
```

```python
from contextlib import ExitStack

import numpy as np

import concourse.bass as bass
from concourse import mybir

F32 = mybir.dt.float32
I32 = mybir.dt.int32
ALU = mybir.AluOpType
ACT = mybir.ActivationFunctionType
AX_X = mybir.AxisListType.X

P = 128
STEPS = 8
NEUR = 256
E = 128
HEADS, DH = 8, 64
NT = STEPS * NEUR // P
NPT = P // STEPS
HALVES = NEUR // P
SB = 2
CH = STEPS // SB
FEAT = 2 * 2 * DH
XW = 2 * DH + 2
QW = 4
NQ = P // 32
COMP = 2 * HEADS * STEPS + 3 * HEADS
OFF_SUM, OFF_BETA = 2 * HEADS * STEPS, 2 * HEADS * STEPS + 2 * HEADS
GE = 160
HID = 3 * GE
GIN = 8
DT = 0.001
EPS = 1e-5
ROUND = 12582912.0
C_ID, C_M16, C_M4, C_CAUS, C_RAMP, C_IOTA = 0, 128, 144, 148, 212, 276
C_ALL = 292
SOLVE_LINKS, BACK_LINKS = 41, 24


def av(t, off, *dims, parts=P, p0=0):
    a = t[:]
    step = a.ap[0][0]
    return bass.AP(a.tensor, a.offset + p0 * step + off, [[step, parts]] + [list(d) for d in dims])


def build(nc, spk_rows, spk_cols, pre, post, att, wpre, wpost, tpre, tpost, vwT, vb, wqkvT, woT, lng, lnb,
          w1, w2, b2, consts, out):
    ctx = ExitStack()
    with ctx:
        def sb(name, shape, dt=F32):
            return ctx.enter_context(nc.sbuf_tensor(name, shape, dt))

        def sem(name):
            return ctx.enter_context(nc.semaphore(name))

        cst = sb("cst", [P, C_ALL])
        X = sb("X", [P, 2, 2 * HEADS * XW])
        spk_i = X[:, 0, 0:STEPS * NEUR].bitcast(I32)
        vst = sb("vst", [P, NT * HEADS * DH])
        attT = vst[:, 0:2 * NEUR * STEPS]
        spk_f = vst[:, 2 * NEUR * STEPS:3 * NEUR * STEPS]
        spk_m = vst[:, 3 * NEUR * STEPS:4 * NEUR * STEPS]
        col_i = sb("col_i", [P, HALVES * STEPS], I32)
        col_f = sb("col_f", [P, HALVES * STEPS])
        col_m = sb("col_m", [P, HALVES * STEPS])
        lat = sb("lat", [P, 4, HALVES * NEUR])
        F = sb("F", [P, 2, 2 * HEADS * FEAT])
        parts = iter(F[:].rearrange("p u (n w) -> p (u n) w", w=SB * NEUR)[:, n, :] for n in range(16))
        trace = [[next(parts) for _ in range(3)] for _ in range(2)]
        inc_pre, dec_post, new_pre, anew = ([next(parts), next(parts)] for _ in range(4))
        new_post, mix = next(parts), next(parts)
        vw = sb("vw", [P, 2, E])
        vbias = sb("vbias", [P, 1])
        wqkv = sb("wqkv", [P, HEADS * (3 * DH + 1)])
        wo = sb("wo", [P, 4, E])
        gam = sb("gam", [P, E])
        bet = sb("bet", [P, E])
        hT = sb("hT", [P, 2, 512])
        h_st = sb("h_st", [P, 2, 512])
        x_st = sb("x_st", [P, 2, 512])
        hb_tok = sb("hb_tok", [P, NT * E])
        x_tok = sb("x_tok", [P, NT * E])
        xT = sb("xT", [P, NT * E])
        stat = sb("stat", [P, 4, 6])
        mv = sb("mv", [P, 2, 4, 2])
        veps = sb("veps", [P, 2, 4])
        rstd = sb("rstd", [P, 2, 4])
        mhalf = sb("mhalf", [P, 4])
        xs = sb("xs", [P, 2, P])
        FT = sb("FT", [P, HEADS, 2, 2, P])
        comp = sb("comp", [P, 2, COMP])
        gmask = sb("gmask", [P, 2 * HEADS * 32])
        cc = sb("cc", [P, STEPS * COMP])
        rsum = sb("rsum", [P, STEPS, 2 * HEADS])
        beta = sb("beta", [P, STEPS, HEADS])
        bk = sb("bk", [P, STEPS, HEADS])
        gn = sb("gn", [P, STEPS * HEADS * STEPS])
        an = sb("an", [P, STEPS * HEADS * STEPS])
        inv = sb("inv", [P, STEPS * HEADS * STEPS])
        prod = sb("prod", [P, HEADS * STEPS * STEPS])
        nn = sb("nn", [P, STEPS * HEADS * STEPS])
        den = sb("den", [P, STEPS * HEADS])
        wc = sb("wc", [P, STEPS * HEADS * STEPS])
        wt = sb("wt", [P, 2, HEADS * STEPS])
        vs = sb("vs", [P, 2, HEADS * DH])
        wexp = sb("wexp", [P, 2, HEADS, P])
        oT = sb("oT", [P, 2, 4, P])
        xa = sb("xa", [P, 2 * E])
        xn = sb("xn", [P, 2 * E])
        h2 = sb("h2", [P, 2 * E])
        z = sb("z", [P, 2 * E])
        fin = sb("fin", [P, 2 * E])
        bits = sb("bits", [P, 2 * 64])
        top = sb("top", [P, 8])
        rem = sb("rem", [P, 8])
        U = sb("U", [P, 2, GIN])
        UT = sb("UT", [GIN, 2, P])
        w1s = sb("w1s", [GIN, 2, HID])
        w2s = sb("w2s", [P, HID])
        b2s = sb("b2s", [P, 3])
        junk = sb("junk", [P, 6, GE])
        opm = sb("opm", [P, 2, 3])
        nop = sb("nop", [P, 2, 3])
        anyop = sb("anyop", [P, 2])
        act2 = sb("act2", [P, 2])
        y = sb("y", [P, 12])
        res = sb("res", [P, 4])
        hot = sb("hot", [P, 64])
        comp_d = nc.dram_tensor("comp_scratch", (NT * P, COMP), F32, kind="Internal").ap()
        w_d = nc.dram_tensor("w_scratch", (NT * P, HEADS * STEPS), F32, kind="Internal").ap()

        pqk = ctx.enter_context(nc.psum_tensor("pqk", [P, 1024], F32))
        pv = ctx.enter_context(nc.psum_tensor("pv", [P, 512], F32))
        ptr = ctx.enter_context(nc.psum_tensor("ptr", [P, 2, 512], F32))
        pgr = ctx.enter_context(nc.psum_tensor("pgr", [P, 2, 512], F32))
        pms = ctx.enter_context(nc.psum_tensor("pms", [P, 512], F32))
        ident = cst[:, C_ID:C_ID + P]

        s_cst, s_tau, s_wgt, s_spk, s_w = (sem(n) for n in (
            "consts_in", "taus_in", "latent_weights_in", "spikes_in", "weights_in"))
        s_trace = [sem("trace_in0"), sem("trace_in1")]
        s_exp = sem("latent_exp_done")
        s_lat = sem("latents_ready")
        s_dve = sem("vector_step")
        s_prod, s_pre = sem("pool_products"), sem("traces_decayed")
        s_anew, s_atr, s_aev = sem("attention_new"), sem("attention_transposed"), sem("attention_evacuated")
        s_hmm, s_hev, s_htr, s_htok = sem("h_product"), sem("h_evacuated"), sem("h_transposed"), sem("h_in_tokens")
        s_var, s_rstd, s_hb = sem("variance_ready"), sem("rstd_ready"), sem("h_plus_bias_ready")
        s_x, s_xtr, s_xT = sem("x_ready"), sem("x_transposed"), sem("xT_ready")
        s_xs, s_qk, s_v = sem("x_staged"), sem("qk_product"), sem("v_product")
        s_relu, s_vev = sem("relu_done"), sem("v_evacuated")
        s_f, s_ftr, s_fev = sem("features_ready"), sem("features_transposed"), sem("features_evacuated")
        s_gram, s_comp = sem("gram_ready"), sem("blocks_ready")
        s_cout = [sem("blocks_stored0"), sem("blocks_stored1")]
        s_cin, s_wc, s_wout = sem("blocks_loaded"), sem("mix_weights_solved"), sem("mix_weights_stored")
        s_bload, s_wexp = sem("back_tiles_loaded"), sem("mix_weights_expanded")
        s_oT, s_oTs, s_y, s_xa = sem("out_product"), sem("out_evacuated"), sem("wo_product"), sem("residual_added")
        s_bvar, s_brstd = sem("back_variance"), sem("back_rstd")
        s_u, s_ut, s_uts = sem("mlp_in_ready"), sem("mlp_in_transposed"), sem("mlp_in_evacuated")
        s_hid, s_mlp = sem("hidden_ready"), sem("hidden_used")
        s_res, s_out = sem("result_ready"), sem("result_stored")
        s_settled = sem("wait_carried")

        block = ctx.enter_context(nc.Block())

        def settled(eng):
            eng.sem_inc(s_settled, 1)

        @block.sync
        def _(sp):
            for credit_of, n in ((s_anew, 2), (s_atr, 2), (s_aev, 2), (s_hev, 2), (s_htr, 2), (s_htok, 2), (s_v, 2),
                                 (s_relu, 1), (s_vev, 1), (s_f, 32), (s_ftr, 16), (s_fev, 2), (s_comp, 2),
                                 (s_cout[0], 16), (s_cout[1], 16), (s_wc, 1), (s_wout, 16), (s_hb, 1), (s_xT, 1),
                                 (s_oT, 1), (s_y, 1), (s_oTs, 1), (s_wexp, 1), (s_xa, 1), (s_hid, 1), (s_ut, 1),
                                 (s_uts, 1), (s_mlp, 1), (s_out, 16)):
                sp.sem_inc(credit_of, n)
            sp.dma_start(lat[:, 2, :], tpre.rearrange("(f p) j -> p f j", p=P)).then_inc(s_tau, 16)
            sp.dma_start(lat[:, 3, :], tpost.rearrange("(f p) j -> p f j", p=P)).then_inc(s_tau, 16)
            sp.dma_start(lat[:, 0, :], wpre.rearrange("(f p) j -> p f j", p=P)).then_inc(s_wgt, 16)
            sp.dma_start(lat[:, 1, :], wpost.rearrange("(f p) j -> p f j", p=P)).then_inc(s_wgt, 16)
            with sp.Fori(0, HALVES) as hf:
                for k in range(CH):
                    sp.wait_ge(s_anew, hf * CH + k + 1)
                    settled(sp)
                    for n, src in enumerate((pre, post, att)):
                        sp.dma_start(trace[k % 2][n].rearrange("p (b j) -> p b j", b=SB),
                                     src[SB * k:SB * k + SB, bass.ds(hf * P, P), :].rearrange("b p j -> p b j")
                                     ).then_inc(s_trace[k % 2], 16)
            with sp.Fori(0, NT // 2) as m:
                t0 = m * 2
                for u in range(2):
                    sp.wait_ge(s_comp, t0 + (u + 1 + 2))
                    settled(sp)
                    sp.wait_ge(s_vev, t0 + (u + 1 + 1))
                    settled(sp)
                    sp.dma_start(comp_d[bass.ds((t0 + u) * P, P), :], comp[:, u, :]).then_inc(s_cout[u], 16)
            with sp.Fori(0, HALVES) as hf:
                for u in range(2):
                    sp.wait_ge(s_cout[u], hf * 64 + (64 + 16))
                    settled(sp)
                sp.wait_ge(s_wc, hf + 1)
                settled(sp)
                sp.dma_start(cc[:], comp_d[bass.ds(hf * (NT * P // 2), NT * P // 2), :].rearrange(
                    "(p s) c -> p (s c)", s=STEPS)).then_inc(s_cin, 16)
                sp.wait_ge(s_wc, hf + 2)
                settled(sp)
                sp.dma_start(w_d[bass.ds(hf * (NT * P // 2), NT * P // 2), :].rearrange(
                    "(p s) c -> p (s c)", s=STEPS), wc[:]).then_inc(s_wout, 16)
            sp.wait_ge(s_wout, 16 + 16 * HALVES)
            with sp.Fori(0, NT // 2) as pr:
                sp.wait_ge(s_wexp, pr * 2 + 1)
                settled(sp)
                sp.wait_ge(s_oT, pr * 2 + 1)
                settled(sp)
                for u in range(2):
                    sp.dma_start(wt[:, u, :], w_d[bass.ds((pr * 2 + u) * P, P), :]).then_inc(s_bload, 16)
                    sp.dma_start(vs[:, u, :], av(vst, (pr * 2 + u) * 512, [1, 512])).then_inc(s_bload, 16)
                sp.wait_ge(s_res, pr + 1)
                settled(sp)
                for u in range(2):
                    sp.dma_start(out[:, bass.ds((pr * 2 + u) * NPT, NPT), :].rearrange("t i e -> i t e"),
                                 fin[:, u * E:(u + 1) * E]).then_inc(s_out, 16)
            sp.wait_ge(s_out, 16 * NT + 16)

        @block.gpsimd
        def _(pool):
            pool.dma_start(spk_i, spk_rows.partition_broadcast(P)).then_inc(s_spk, 16)
            pool.dma_start(col_i[:], spk_cols.rearrange("(f p) b -> p f b", p=P)).then_inc(s_spk, 16)
            pool.dma_start(cst[:], consts).then_inc(s_cst, 16)
            pool.dma_start(vw[:], vwT.rearrange("(c p) e -> p c e", p=P)).then_inc(s_w, 16)
            pool.dma_start(vbias[:], vb).then_inc(s_w, 16)
            pool.dma_start(wqkv[:], wqkvT).then_inc(s_w, 16)
            pool.dma_start(wo[:], woT.rearrange("(c p) e -> p c e", p=P)).then_inc(s_w, 16)
            pool.dma_start(gam[:], lng.partition_broadcast(P)).then_inc(s_w, 16)
            pool.dma_start(bet[:], lnb.partition_broadcast(P)).then_inc(s_w, 16)
            pool.dma_start(w1s[:], w1.rearrange("r k n -> k r n")).then_inc(s_w, 16)
            pool.dma_start(w2s[:], w2.partition_broadcast(P)).then_inc(s_w, 16)
            pool.dma_start(b2s[:], b2.partition_broadcast(P)).then_inc(s_w, 16)
            pool.wait_ge(s_lat, 1)
            with pool.Fori(0, HALVES) as hf:
                for k in range(CH):
                    u = k % 2
                    c = hf * CH + k
                    pool.wait_ge(s_trace[u], hf * (48 * CH // 2) + 48 * (k // 2 + 1))
                    pool.wait_ge(s_anew, c + 1)
                    settled(pool)
                    nc.gpsimd.tensor_tensor(new_pre[u].rearrange("p (b j) -> p b j", b=SB),
                                            trace[u][0].rearrange("p (b j) -> p b j", b=SB),
                                            av(lat, hf * NEUR + 2 * 512, [0, SB], [1, NEUR]), ALU.mult)
                    nc.gpsimd.tensor_tensor(inc_pre[u].rearrange("p (b j) -> p b j", b=SB),
                                            av(spk_f, SB * k * NEUR, [NEUR, SB], [1, NEUR]),
                                            av(lat, hf * NEUR, [0, SB], [1, NEUR]), ALU.mult).then_inc(s_prod, 1)
                    pool.wait_ge(s_prod, c + 1)
                    nc.gpsimd.tensor_tensor(new_pre[u], new_pre[u], inc_pre[u], ALU.add)
                    nc.gpsimd.tensor_tensor(dec_post[u].rearrange("p (b j) -> p b j", b=SB),
                                            trace[u][1].rearrange("p (b j) -> p b j", b=SB),
                                            av(lat, hf * NEUR + 3 * 512, [0, SB], [1, NEUR]),
                                            ALU.mult).then_inc(s_pre, 1)
            pool.wait_ge(s_w, 16 * 9)
            with pool.Fori(0, 2) as m:
                g0 = m * 2
                for u in range(2):
                    pool.wait_ge(s_var, g0 + (u + 1))
                    nc.gpsimd.tensor_tensor(rstd[:, u, :], veps[:, u, :], mhalf[:], ALU.pow).then_inc(s_rstd, 1)
                    nc.gpsimd.tensor_tensor(av(hb_tok, (g0 + u) * 512, [E, 4], [1, E]),
                                            h_st[:, u, :].rearrange("p (t e) -> p t e", e=E),
                                            av(bet, 0, [0, 4], [1, E]), ALU.add).then_inc(s_hb, 1)
            with pool.Fori(0, NT // 2) as pr:
                pool.wait_ge(s_bload, pr * 64 + 64)
                for u in range(2):
                    pool.wait_ge(s_oT, pr * 2 + 1)
                    nc.gpsimd.tensor_tensor(wexp[:, u].rearrange("p h (i t) -> p h i t", t=STEPS),
                                            av(wt, u * 64, [STEPS, HEADS], [0, NPT], [1, STEPS]),
                                            av(cst, C_M16, [0, HEADS], [1, NPT], [0, STEPS]),
                                            ALU.mult).then_inc(s_wexp, 1)
                for n in range(2):
                    pool.wait_ge(s_bvar, pr * 2 + (n + 1))
                    nc.gpsimd.tensor_tensor(rstd[:, n, 0:2], veps[:, n, 0:2], mhalf[:, 0:2],
                                            ALU.pow).then_inc(s_brstd, 1)

        @block.scalar
        def _(act):
            act.wait_ge(s_tau, 32)
            nc.scalar.activation(lat[:, 2:4, :], lat[:, 2:4, :], ACT.Exp, scale=-1.0).then_inc(s_exp, 1)
            act.wait_ge(s_exp, 1)
            nc.scalar.activation(lat[:, 2:4, :], lat[:, 2:4, :], ACT.Exp, scale=-DT).then_inc(s_exp, 1)
            act.wait_ge(s_wgt, 32)
            nc.scalar.activation(lat[:, 0:2, :], lat[:, 0:2, :], ACT.Exp).then_inc(s_exp, 1)
            with act.Fori(0, HALVES) as hf:
                for k in range(CH):
                    act.wait_ge(s_atr, hf * CH + (k + 1 + 2))
                    for b in range(SB):
                        last = nc.scalar.activation(
                            av(attT, hf * (P * STEPS) + SB * k + b, [NEUR * STEPS, 2], [STEPS, P]),
                            ptr[:, k % 2, b * NEUR:(b + 1) * NEUR].rearrange("p (c i) -> p c i", c=2), ACT.Copy)
                    last.then_inc(s_aev, 1)
            act.wait_ge(s_w, 16 * 9)
            with act.Fori(0, 2) as m:
                g0 = m * 2
                for u in range(2):
                    g = g0 + u
                    act.wait_ge(s_hmm, g + 1)
                    act.wait_ge(s_htr, g + 1)
                    nc.scalar.activation(hT[:, u, :], pgr[:, u, :], ACT.Identity, bias=vbias[:]).then_inc(s_hev, 1)
                    act.wait_ge(s_x, g + 1)
                    nc.scalar.activation(av(x_tok, g * 512, [1, 512]), x_st[:, u, :], ACT.Copy)
                    act.wait_ge(s_xtr, g + 1)
                    nc.scalar.activation(av(xT, g * 512, [1, 512]), pqk[:, u * 512:(u + 1) * 512],
                                         ACT.Copy).then_inc(s_xT, 1)

            def stage(t, u):
                act.wait_ge(s_v, t + 1)
                nc.scalar.activation(xs[:, u, :], av(xT, t * P, [1, P]), ACT.Copy).then_inc(s_xs, 1)

            def evacuate_qkv(t, u):
                act.wait_ge(s_qk, t + 1)
                act.wait_ge(s_f, t * 16 + 16)
                xv = X[:, u, :].rearrange("p (j w) -> p j w", w=XW)
                qk = pqk[:].rearrange("p (j d) -> p j d", d=DH)
                nc.scalar.activation(xv[:, :, 2:2 + DH], qk, ACT.Relu)
                nc.scalar.activation(xv[:, :, 2 + DH:XW], qk, ACT.Relu, scale=-1.0)
                nc.scalar.activation(xv[:, :, 0:2], qk[:, :, DH - 2:DH], ACT.Relu, scale=-1.0).then_inc(s_relu, 1)
                act.wait_ge(s_v, t + (1 + 2))
                nc.scalar.activation(av(vst, t * 512, [1, 512]), pv[:], ACT.Copy)
                act.wait_ge(s_cout[u], (t - u) * 8 + 16)
                nc.scalar.activation(comp[:, u, OFF_BETA:COMP], pms[:, 0:HEADS], ACT.Exp,
                                     scale=-1.0).then_inc(s_vev, 1)

            def evacuate_features(t):
                for h in range(HEADS):
                    act.wait_ge(s_ftr, t * 8 + (16 + h + 1))
                    nc.scalar.activation(FT[:, h].rearrange("p r q t -> p (r q t)"), ptr[:, h % 2, :],
                                         ACT.Copy).then_inc(s_fev, 1)

            act.wait_ge(s_xT, 4 + 1)
            stage(0, 0)
            stage(1, 1)
            evacuate_qkv(0, 0)
            with act.Fori(0, NT // 2 - 1) as m:
                t0 = m * 2
                for u in range(2):
                    evacuate_qkv(t0 + (u + 1), 1 - u)
                    stage(t0 + (u + 2), u)
                    evacuate_features(t0 + u)
            evacuate_qkv(NT - 1, 1)
            evacuate_features(NT - 2)
            evacuate_features(NT - 1)

            with act.Fori(0, NT // 2) as pr:
                for u in range(2):
                    act.wait_ge(s_oT, pr * 2 + (u + 2))
                    act.wait_ge(s_y, pr * 2 + 1)
                    nc.scalar.activation(oT[:, u].rearrange("p c t -> p (c t)"), ptr[:, u, :],
                                         ACT.Copy).then_inc(s_oTs, 1)
                act.wait_ge(s_ut, pr + 2)
                act.wait_ge(s_hid, pr * 2 + 1)
                nc.scalar.activation(UT[:].rearrange("k u t -> k (u t)"), pv[0:GIN, 0:2 * P],
                                     ACT.Copy).then_inc(s_uts, 1)

        @block.vector
        def _(dve):
            count = [0, 0]

            def link(ins):
                ins.then_inc(s_dve, 1)
                count[1] += 1
                dve.wait_ge(s_dve, count[0] + count[1])

            nc.vector.memset(mhalf[:], -0.5)
            nc.vector.memset(U[:], 1.0)
            nc.vector.memset(inv[:], 0.0)
            link(nc.vector.memset(nn[:], 0.0))
            nc.vector.memset(av(inv, 0, [65, STEPS], [8, HEADS]), 1.0)
            dve.wait_ge(s_spk, 32)
            nc.vector.tensor_copy(spk_f, spk_i)
            nc.vector.tensor_scalar(spk_m, spk_i, 0.0, None, ALU.not_equal)
            nc.vector.tensor_copy(col_f[:], col_i[:])
            nc.vector.tensor_scalar(col_m[:], col_i[:], 0.0, None, ALU.not_equal)
            dve.wait_ge(s_exp, 3)
            link(nc.vector.tensor_scalar(lat[:, 0:2, :], lat[:, 0:2, :], DT, None, ALU.mult))
            nc.vector.memset(rstd[:], 0.0).then_inc(s_lat, 1)
            before = count[1]
            with dve.Fori(0, HALVES) as hf:
                for k in range(CH):
                    count[0] = hf * (6 * CH)
                    u = k % 2
                    c = hf * CH + k
                    dve.wait_ge(s_trace[u], hf * (48 * CH // 2) + 48 * (k // 2 + 1))
                    dve.wait_ge(s_pre, c + 1)

                    def halves(out_, in0, col, in1, in0_fixed=None):
                        for b in range(SB):
                            js = slice(b * NEUR, (b + 1) * NEUR)
                            last = nc.vector.scalar_tensor_tensor(
                                out_[:, js], in0_fixed if in0_fixed is not None else in0[:, js],
                                av(col, hf * STEPS + SB * k + b, [1, 1]), in1[:, js], ALU.mult, ALU.add)
                        return last

                    np_, dp, atn = new_pre[u], dec_post[u], trace[u][2]
                    link(halves(new_post, None, col_f, dp, av(lat, hf * NEUR + 512, [1, NEUR])))
                    link(nc.vector.tensor_tensor(mix, new_post, spk_m[:, SB * k * NEUR:SB * (k + 1) * NEUR],
                                                 ALU.mult))
                    link(halves(mix, np_, col_m, mix))
                    link(nc.vector.tensor_tensor(new_post, atn, mix, ALU.mult))
                    link(nc.vector.tensor_tensor(new_post, atn, new_post, ALU.subtract))
                    dve.wait_ge(s_atr, c + 1)
                    link(halves(anew[u], np_, col_m, new_post))
                    nc.vector.tensor_scalar(anew[u], anew[u], -0.5, 1.5, ALU.max,
                                            ALU.min).then_inc(s_anew, 1)
            assert count[1] - before == 6 * CH
            count[:] = [0, before + 6 * CH * HALVES]

            before = count[1]
            with dve.Fori(0, 2) as m:
                g0 = m * 2
                for u in range(2):
                    count[0] = g0
                    g = g0 + u
                    dve.wait_ge(s_htr, g + (1 + 2))
                    dve.wait_ge(s_hb, g0 + 1)
                    nc.vector.tensor_copy(h_st[:, u, :], ptr[:, u, :])
                    for t in range(4):
                        last = nc.vector.bn_stats(stat[:, t, :], ptr[:, u, t * E:(t + 1) * E])
                    last.then_inc(s_htok, 1)
                    dve.wait_ge(s_htok, g + (1 + 2))
                    settled(dve)
                    for t in range(4):
                        last = nc.vector.bn_aggr(mv[:, u, t, :], stat[:, t, :])
                    link(last)
                    nc.vector.tensor_scalar(veps[:, u, :], mv[:, u, :, 1], EPS, None, ALU.add).then_inc(s_var, 1)
                    dve.wait_ge(s_rstd, g + 1)
                    dve.wait_ge(s_xT, g0 + 1)
                    for t in range(4):
                        last = nc.vector.tensor_scalar(x_st[:, u, t * E:(t + 1) * E], h_st[:, u, t * E:(t + 1) * E],
                                                       mv[:, u, t, 0:1], rstd[:, u, t:t + 1], ALU.subtract, ALU.mult)
                    last.then_inc(s_x, 1)
            assert count[1] - before == 2
            count[:] = [0, before + 4]

            def features(t, u):
                dve.wait_ge(s_relu, t + (1 + 1))
                dve.wait_ge(s_ftr, t * 8 + 8)
                dve.wait_ge(s_cout[u], (t - u) * 8 + 16)
                for j in range(2 * HEADS):
                    base = u * 2 * HEADS * XW + j * XW
                    nc.vector.scalar_tensor_tensor(
                        F[:, u, j * FEAT:(j + 1) * FEAT].rearrange("p (r d) -> p r d", r=2),
                        av(X, base + 2, [0, 2], [1, 2 * DH]), 1.0, av(X, base, [1, 2], [1, 2 * DH]),
                        ALU.mult, ALU.mult,
                        accum_out=comp[:, u, OFF_SUM + j:OFF_SUM + j + 1]).then_inc(s_f, 1)

            def blocks(t, u):
                dve.wait_ge(s_comp, t + 2)
                dve.wait_ge(s_gram, t + 1)
                link(nc.vector.tensor_tensor(gmask[:].rearrange("p (j i t) -> p j i t", i=QW, t=STEPS),
                                             pgr[:, u, :].rearrange("p (j i t) -> p j i t", i=QW, t=STEPS),
                                             av(cst, C_M4, [0, 2 * HEADS], [1, QW], [0, STEPS]), ALU.mult))
                nc.vector.tensor_reduce(comp[:, u, 0:OFF_SUM].rearrange("p (j t) -> p j t", t=STEPS),
                                        av(gmask, 0, [32, 2 * HEADS], [1, STEPS], [STEPS, QW]), AX_X,
                                        ALU.add).then_inc(s_comp, 1)

            features(0, 0)
            before = count[1]
            with dve.Fori(0, NT // 2 - 1) as m:
                t0 = m * 2
                for u in range(2):
                    count[0] = t0
                    features(t0 + (u + 1), 1 - u)
                    blocks(t0 + u, u)
            assert count[1] - before == 2
            count[:] = [0, before + NT - 2]
            features(NT - 1, 1)
            blocks(NT - 2, 0)
            blocks(NT - 1, 1)

            T3 = STEPS * HEADS
            before = count[1]
            with dve.Fori(0, HALVES) as hf:
                count[0] = hf * SOLVE_LINKS
                dve.wait_ge(s_cin, hf * 16 + 16)
                ccv = cc[:].rearrange("p (s c) -> p s c", c=COMP)
                nc.vector.reciprocal(rsum[:], ccv[:, :, OFF_SUM:OFF_BETA])
                link(nc.vector.tensor_scalar(beta[:], ccv[:, :, OFF_BETA:COMP], 1.0, None, ALU.add))
                link(nc.vector.reciprocal(beta[:], beta[:]))
                rk = av(rsum, 0, [0, STEPS], [2, HEADS], [2 * HEADS, STEPS])
                link(nc.vector.tensor_tensor(bk[:], beta[:], av(rsum, 0, [2 * HEADS, STEPS], [2, HEADS]), ALU.mult))
                d3 = dict(t=STEPS, h=HEADS)
                gv = gn[:].rearrange("p (t h s) -> p t h s", **d3)
                an_v = an[:].rearrange("p (t h s) -> p t h s", **d3)
                nc.vector.tensor_tensor(gv, av(cc, 0, [1, STEPS], [16, HEADS], [COMP, STEPS]), rk, ALU.mult)
                link(nc.vector.tensor_tensor(an_v, av(cc, 8, [1, STEPS], [16, HEADS], [COMP, STEPS]), rk, ALU.mult))
                nc.vector.tensor_tensor(gv, gv, av(bk, 0, [HEADS, STEPS], [1, HEADS], [0, STEPS]), ALU.mult)
                link(nc.vector.tensor_tensor(an_v, an_v, av(rsum, 1, [2 * HEADS, STEPS], [2, HEADS], [0, STEPS]),
                                             ALU.mult))
                link(nc.vector.tensor_tensor(an_v, an_v, av(cst, C_CAUS, [STEPS, STEPS], [0, HEADS], [1, STEPS]),
                                             ALU.mult))
                link(nc.vector.tensor_reduce(den[:], an[:].rearrange("p (a s) -> p a s", s=STEPS), AX_X, ALU.add))
                link(nc.vector.tensor_scalar(den[:], den[:], EPS, None, ALU.add))
                link(nc.vector.reciprocal(den[:], den[:]))
                link(nc.vector.tensor_scalar(den[:], den[:], float(DH) ** -0.5, None, ALU.mult))

                def row(dst, coef, t, n, negate):
                    pr_ = av(prod, 0, [n * n, HEADS], [n, n], [1, n])
                    link(nc.vector.tensor_tensor(pr_, av(inv, 0, [8, HEADS], [1, n], [T3, n]),
                                                 av(coef, t * T3, [8, HEADS], [0, n], [1, n]), ALU.mult))
                    link(nc.vector.tensor_reduce(av(dst, t * T3, [8, HEADS], [1, n]), pr_, AX_X, ALU.add,
                                                 negate=negate))

                for t in range(1, STEPS):
                    row(inv, gn, t, t, True)
                for t in range(STEPS):
                    row(nn, an, t, t + 1, False)
                dve.wait_ge(s_wout, hf * 16 + 16)
                link(nc.vector.tensor_tensor(nn[:].rearrange("p (a u) -> p a u", u=STEPS),
                                             nn[:].rearrange("p (a u) -> p a u", u=STEPS),
                                             av(den, 0, [1, STEPS * HEADS], [0, STEPS]), ALU.mult))
                nc.vector.tensor_tensor(wc[:].rearrange("p (u h t) -> p u h t", u=STEPS, h=HEADS),
                                        av(nn, 0, [1, STEPS], [8, HEADS], [T3, STEPS]),
                                        av(beta, 0, [HEADS, STEPS], [1, HEADS], [0, STEPS]),
                                        ALU.mult).then_inc(s_wc, 1)
            assert count[1] - before == SOLVE_LINKS, count[1] - before
            count[:] = [0, before + SOLVE_LINKS * HALVES]

            def w2v(t):
                return t[:].rearrange("p (u e) -> p u e", u=2)

            before = count[1]
            with dve.Fori(0, NT // 2) as pr:
                count[0] = pr * BACK_LINKS

                def normalise(src, dst, n):
                    for u in range(2):
                        last = nc.vector.bn_stats(stat[:, u, :], src[:, u * E:(u + 1) * E])
                    link(last)
                    settled(dve)
                    for u in range(2):
                        last = nc.vector.bn_aggr(mv[:, 0, u, :], stat[:, u, :])
                    link(last)
                    nc.vector.tensor_scalar(veps[:, n, 0:2], mv[:, 0, 0:2, 1], EPS, None, ALU.add).then_inc(s_bvar, 1)
                    dve.wait_ge(s_brstd, pr * 2 + (n + 1))
                    for u in range(2):
                        last = nc.vector.tensor_scalar(dst[:, u * E:(u + 1) * E], src[:, u * E:(u + 1) * E],
                                                       mv[:, 0, u, 0:1], rstd[:, n, u:u + 1], ALU.subtract, ALU.mult)
                    link(last)

                dve.wait_ge(s_y, pr * 2 + 3)
                nc.vector.tensor_tensor(xa[:], av(x_tok, pr * 2 * E, [1, 2 * E]), pms[:, 0:2 * E],
                                        ALU.add).then_inc(s_xa, 1)
                dve.wait_ge(s_xa, pr + 2)
                normalise(xa, xn, 0)
                link(nc.vector.tensor_tensor(w2v(xn), w2v(xn), av(gam, 0, [0, 2], [1, E]), ALU.mult))
                link(nc.vector.tensor_tensor(h2[:], xn[:], av(hb_tok, pr * 2 * E, [1, 2 * E]), ALU.add))
                normalise(h2, z, 1)
                link(nc.vector.scalar_tensor_tensor(w2v(bits), av(z, 16, [E, 2], [1, 64]), 0.5,
                                                    av(cst, C_RAMP, [0, 2], [1, 64]), ALU.is_gt, ALU.mult))
                link(nc.vector.tensor_reduce(top[:], bits[:].rearrange("p (n b) -> p n b", b=16), AX_X, ALU.max))
                link(nc.vector.tensor_scalar(rem[:], top[:], -1.0, 16.0, ALU.mult, ALU.add))
                dve.wait_ge(s_ut, pr + 1)
                nc.vector.scalar_tensor_tensor(U[:, :, 0:4], top[:].rearrange("p (u n) -> p u n", u=2), 0.0,
                                               rem[:].rearrange("p (u n) -> p u n", u=2), ALU.is_gt, ALU.mult)
                nc.vector.tensor_copy(U[:, :, 4:7], av(z, 1, [E, 2], [1, 3])).then_inc(s_u, 1)
                link(nc.vector.tensor_scalar(opm[:], av(z, 1, [E, 2], [1, 3]), 0.5, None, ALU.is_gt))
                nc.vector.tensor_reduce(anyop[:], opm[:], AX_X, ALU.max)
                link(nc.vector.tensor_scalar(nop[:], opm[:], -1.0, 1.0, ALU.mult, ALU.add))
                nc.vector.tensor_tensor(opm[:, :, 1], opm[:, :, 1], nop[:, :, 0], ALU.mult)
                nc.vector.tensor_tensor(opm[:, :, 2], nop[:, :, 0], nop[:, :, 1], ALU.mult)
                link(nc.vector.tensor_scalar(act2[:], av(z, 0, [E, 2]), 0.5, 2.0, ALU.is_ge, ALU.mult))
                link(nc.vector.tensor_tensor(act2[:], act2[:], anyop[:], ALU.mult))
                for u in range(2):
                    dve.wait_ge(s_hid, pr * 2 + (u + 2))
                    for r in range(2):
                        for op in range(3):
                            last = nc.vector.scalar_tensor_tensor(
                                junk[:, r * 3 + op, :], pqk[:, r * 512 + op * GE:r * 512 + (op + 1) * GE], 0.0,
                                w2s[:, op * GE:(op + 1) * GE], ALU.max, ALU.mult,
                                accum_out=y[:, u * 6 + r * 3 + op:u * 6 + r * 3 + op + 1])
                    last.then_inc(s_mlp, 1)
                dve.wait_ge(s_mlp, pr * 2 + 3)
                link(nc.vector.tensor_tensor(y[:].rearrange("p (a o) -> p a o", o=3),
                                             y[:].rearrange("p (a o) -> p a o", o=3),
                                             av(b2s, 0, [0, 4], [1, 3]), ALU.add))
                link(nc.vector.tensor_tensor(y[:].rearrange("p (u r o) -> p u r o", r=2, o=3),
                                             y[:].rearrange("p (u r o) -> p u r o", r=2, o=3),
                                             av(opm, 0, [3, 2], [0, 2], [1, 3]), ALU.mult))
                link(nc.vector.tensor_reduce(res[:], y[:].rearrange("p (a o) -> p a o", o=3), AX_X, ALU.add))
                link(nc.vector.tensor_scalar(res[:], res[:], -1.0, 16.0, ALU.max, ALU.min))
                link(nc.vector.tensor_scalar(res[:], res[:], ROUND, ROUND, ALU.add, ALU.subtract))
                link(nc.vector.tensor_scalar(res[:], res[:], 0.0, 15.0, ALU.max, ALU.min))
                link(nc.vector.tensor_tensor(hot[:].rearrange("p (a k) -> p a k", k=16),
                                             av(cst, C_IOTA, [0, 4], [1, 16]), av(res, 0, [1, 4], [0, 16]),
                                             ALU.is_equal))
                link(nc.vector.tensor_tensor(w2v(hot), w2v(hot), av(act2, 0, [1, 2], [0, 32]), ALU.mult))
                link(nc.vector.tensor_tensor(av(z, 80, [E, 2], [1, 32]), av(z, 80, [E, 2], [1, 32]), w2v(hot), ALU.add))
                dve.wait_ge(s_out, pr * 32 + 16)
                nc.vector.tensor_tensor(fin[:], h2[:], z[:], ALU.add).then_inc(s_res, 1)
            assert count[1] - before == BACK_LINKS, count[1] - before

        @block.tensor
        def _(pe):
            mm, tr = nc.tensor.matmul, nc.tensor.transpose
            pe.wait_ge(s_cst, 16)
            with pe.Fori(0, HALVES) as hf:
                for k in range(CH):
                    c = hf * CH + k
                    pe.wait_ge(s_anew, c + (1 + 2))
                    pe.wait_ge(s_aev, c + 1)
                    for n in range(4):
                        last = tr(ptr[:, k % 2, n * P:(n + 1) * P], anew[k % 2][:, n * P:(n + 1) * P], ident)
                    last.then_inc(s_atr, 1)
            pe.wait_ge(s_aev, HALVES * CH + 2)
            pe.wait_ge(s_w, 16 * 9)
            with pe.Fori(0, 2) as m:
                g0 = m * 2
                for u in range(2):
                    g = g0 + u
                    pe.wait_ge(s_hev, g + 1)
                    for c in range(2):
                        last = mm(pgr[:, u, :], vw[:, c, :], av(attT, g * 512 + c * NEUR * STEPS, [1, 512]),
                                  start=(c == 0), stop=(c == 1))
                    last.then_inc(s_hmm, 1)
                    pe.wait_ge(s_hev, g + (1 + 2))
                    pe.wait_ge(s_htok, g + 1)
                    for t in range(4):
                        last = tr(ptr[:, u, t * P:(t + 1) * P], hT[:, u, t * P:(t + 1) * P], ident)
                    last.then_inc(s_htr, 1)
                    pe.wait_ge(s_x, g + 1)
                    pe.wait_ge(s_xT, g0 + 1)
                    for t in range(4):
                        last = tr(pqk[:, u * 512 + t * P:u * 512 + (t + 1) * P], x_st[:, u, t * P:(t + 1) * P], ident)
                    last.then_inc(s_xtr, 1)

            def project(t, u):
                pe.wait_ge(s_xs, t + 1)
                pe.wait_ge(s_relu, t + 1)
                for n in range(2):
                    last = mm(pqk[:, n * 512:(n + 1) * 512], xs[:, u, :], wqkv[:, n * 512:(n + 1) * 512],
                              start=True, stop=True)
                last.then_inc(s_qk, 1)
                pe.wait_ge(s_vev, t + 1)
                mm(pv[:], xs[:, u, :], wqkv[:, 1024:1536], start=True, stop=True)
                mm(pms[:, 0:HEADS], xs[:, u, :], wqkv[:, 1536:1544], start=True, stop=True).then_inc(s_v, 1)

            def gram(t, u, h):
                pe.wait_ge(s_fev, t * 8 + (h + 1 + 2))
                if h == 0:
                    pe.wait_ge(s_comp, t + 1)
                for g in range(NQ):
                    for r in range(2):
                        last = mm(pgr[32 * g:32 * g + 32, u, h * 64:(h + 1) * 64], FT[:, h, r, 0, 32 * g:32 * g + 32],
                                  av(FT, h * 512 + r * 256 + 32 * g, [P, 2], [1, 32]), start=(r == 0), stop=(r == 1))
                if h == HEADS - 1:
                    last.then_inc(s_gram, 1)

            def transpose_and_multiply(t, u):
                for h in range(HEADS):
                    pe.wait_ge(s_f, t * 16 + (32 + 2 * h + 2))
                    pe.wait_ge(s_fev, t * 8 + (h + 1))
                    for r in range(2):
                        for q in range(2):
                            src = (2 * h + q) * FEAT + r * 2 * DH
                            last = tr(ptr[:, h % 2, (2 * r + q) * P:(2 * r + q + 1) * P], F[:, u, src:src + P], ident)
                    last.then_inc(s_ftr, 1)
                    if h:
                        gram(t, u, h - 1)
                gram(t, u, HEADS - 1)

            project(0, 0)
            with pe.Fori(0, NT // 2 - 1) as m:
                t0 = m * 2
                for u in range(2):
                    project(t0 + (u + 1), 1 - u)
                    transpose_and_multiply(t0 + u, u)
            project(NT - 1, 1)
            transpose_and_multiply(NT - 2, 0)
            transpose_and_multiply(NT - 1, 1)

            with pe.Fori(0, NT // 2) as pr:
                for u in range(2):
                    pe.wait_ge(s_wexp, pr * 2 + (u + 2))
                    pe.wait_ge(s_oTs, pr * 2 + 1)
                    for h in range(HEADS):
                        p0 = DH * (h % 2)
                        last = mm(ptr[p0:p0 + DH, u, (h // 2) * P:(h // 2 + 1) * P], vs[:, u, h * DH:(h + 1) * DH],
                                  wexp[:, u, h, :], start=True, stop=True)
                    last.then_inc(s_oT, 1)
                pe.wait_ge(s_xa, pr + 1)
                for u in range(2):
                    pe.wait_ge(s_oTs, pr * 2 + (u + 2))
                    for c in range(4):
                        last = mm(pms[:, u * P:(u + 1) * P], oT[:, u, c, :], wo[:, c, :], start=(c == 0), stop=(c == 3))
                    last.then_inc(s_y, 1)
                pe.wait_ge(s_u, pr + 1)
                pe.wait_ge(s_uts, pr + 1)
                for u in range(2):
                    last = mm(pv[0:GIN, u * P:(u + 1) * P], U[:, u, :], ident, start=True, stop=True)
                last.then_inc(s_ut, 1)
                pe.wait_ge(s_uts, pr + 2)
                for u in range(2):
                    pe.wait_ge(s_mlp, pr * 2 + (u + 1))
                    for r in range(2):
                        last = mm(pqk[:, r * 512:r * 512 + HID], UT[:, u, :], w1s[:, r, :], start=True, stop=True)
                    last.then_inc(s_hid, 1)


def constants():
    c = np.zeros((P, C_ALL), np.float32)
    p = np.arange(P)
    c[p, C_ID + p] = 1
    c[p, C_M16 + p // STEPS] = 1
    c[p, C_M4 + p % 32 // STEPS] = 1
    t = np.arange(STEPS)
    c[:, C_CAUS:C_CAUS + 64] = (t[None, :] <= t[:, None]).astype(np.float32).reshape(-1)
    c[:, C_RAMP:C_RAMP + 64] = np.tile(16 - np.arange(16), 4)
    c[:, C_IOTA:C_IOTA + 16] = np.arange(16)
    return c


def kernel(**inputs):
    import concourse.bacc as bacc
    from concourse.bass_utils import run_bass_kernel_spmd

    a = {k: np.asarray(v) for k, v in inputs.items()}
    ffn = {op: {n: a[f"L0_ffn_{op}_{n}"] for n in ("w1", "b1", "w2", "b2")} for op in ("and", "or", "xor")}
    wh = a["L0_attn_W_qkvb"].reshape(HEADS, 3 * DH + 1, E)
    wqkv = np.concatenate([np.concatenate([wh[:, DH:2 * DH], wh[:, 0:DH]], 1).reshape(-1, E),
                           wh[:, 2 * DH:3 * DH].reshape(-1, E), wh[:, 3 * DH]], 0).T
    w1 = np.zeros((2, GIN, HID), np.float32)
    for n, op in enumerate(ffn.values()):
        cols = slice(n * GE, (n + 1) * GE)
        for r in range(2):
            w1[r, r, cols], w1[r, 2 + r, cols] = op["w1"][0], op["w1"][1]
            w1[r, 4, cols], w1[r, 5, cols], w1[r, 6, cols] = op["w1"][46], op["w1"][44], op["w1"][45]
            w1[r, 7, cols] = op["b1"]
    arrays = {
        "spk_rows": a["x"].reshape(-1), "spk_cols": a["x"].T,
        "pre": a["fside_BSS_pre_trace"], "post": a["fside_BSS_post_trace"], "att": a["fside_BSS_attention"],
        "wpre": a["L0_tok_latent_pre_weight"][0], "wpost": a["L0_tok_latent_post_weight"][0],
        "tpre": a["L0_tok_latent_pre_tau_s"][0], "tpost": a["L0_tok_latent_post_tau_s"][0],
        "vwT": a["L0_tok_v_w"].T, "vb": a["L0_tok_v_b"].reshape(E, 1), "wqkvT": wqkv, "woT": a["L0_attn_W_o"].T,
        "lng": a["L0_attn_ln_g"], "lnb": a["L0_attn_ln_b"], "w1": w1,
        "w2": np.concatenate([op["w2"][:, 64] for op in ffn.values()]),
        "b2": np.concatenate([op["b2"][64:65] for op in ffn.values()]), "consts": constants(),
    }
    arrays = {k: np.ascontiguousarray(v) for k, v in arrays.items()}
    nc = bacc.Bacc("TRN2", target_bir_lowering=False, num_devices=1)
    args = [nc.dram_tensor(k, v.shape, mybir.dt.from_np(v.dtype), kind="ExternalInput").ap()
            for k, v in arrays.items()]
    out = nc.dram_tensor("out", (STEPS, NEUR, E), F32, kind="ExternalOutput").ap()
    build(nc, *args, out)
    return run_bass_kernel_spmd(nc, [arrays], core_ids=[0]).results[0]["out"]
```

```python
from contextlib import ExitStack

import numpy as np

import concourse.bass as bass
from concourse import mybir

F32 = mybir.dt.float32
I32 = mybir.dt.int32
ALU = mybir.AluOpType
ACT = mybir.ActivationFunctionType
AX_X = mybir.AxisListType.X

P = 128
STEPS = 8
NEUR = 256
E = 128
HEADS, DH = 8, 64
NT = STEPS * NEUR // P
NPT = P // STEPS
HALVES = NEUR // P
SB = 2
CH = STEPS // SB
FEAT = 2 * 2 * DH
XW = 2 * DH + 2
QW = 4
NQ = P // 32
COMP = 2 * HEADS * STEPS + 3 * HEADS
OFF_SUM, OFF_BETA = 2 * HEADS * STEPS, 2 * HEADS * STEPS + 2 * HEADS
GE = 160
HID = 3 * GE
GIN = 8
DT = 0.001
EPS = 1e-5
ROUND = 12582912.0
C_ID, C_M16, C_M4, C_CAUS, C_RAMP, C_IOTA = 0, 128, 144, 148, 212, 276
C_ALL = 292
PAIRS = NT // 2
SOLVE_LINKS, BACK_LINKS = 41, 24


def av(t, off, *dims, parts=P, p0=0):
    a = t[:]
    step = a.ap[0][0]
    return bass.AP(a.tensor, a.offset + p0 * step + off, [[step, parts]] + [list(d) for d in dims])


def build(nc, spk_rows, spk_cols, pre, post, att, wpre, wpost, tpre, tpost, vwT, vb, wqkvT, woT, lng, lnb,
          w1, w2, b2, consts, out):
    ctx = ExitStack()
    with ctx:
        def sb(name, shape, dt=F32):
            return ctx.enter_context(nc.sbuf_tensor(name, shape, dt))

        def sem(name):
            return ctx.enter_context(nc.semaphore(name))

        cst = sb("cst", [P, C_ALL])
        X = sb("X", [P, 2, 2 * HEADS * XW])
        spk_i = X[:, 0, 0:STEPS * NEUR].bitcast(I32)
        vst = sb("vst", [P, NT * HEADS * DH])
        attT = vst[:, 0:2 * NEUR * STEPS]
        spk_f = vst[:, 2 * NEUR * STEPS:3 * NEUR * STEPS]
        spk_m = vst[:, 3 * NEUR * STEPS:4 * NEUR * STEPS]
        col_i = sb("col_i", [P, HALVES * STEPS], I32)
        col_f = sb("col_f", [P, HALVES * STEPS])
        col_m = sb("col_m", [P, HALVES * STEPS])
        lat = sb("lat", [P, 4, HALVES * NEUR])
        F = sb("F", [P, 2, 2 * HEADS * FEAT])
        parts = iter(F[:].rearrange("p u (n w) -> p (u n) w", w=SB * NEUR)[:, n, :] for n in range(16))
        trace = [[next(parts) for _ in range(3)] for _ in range(2)]
        inc_pre, dec_post, new_pre, anew = ([next(parts), next(parts)] for _ in range(4))
        new_post, mix = next(parts), next(parts)
        vw = sb("vw", [P, 2, E])
        vbias = sb("vbias", [P, 1])
        wqkv = sb("wqkv", [P, HEADS * (3 * DH + 1)])
        wo = sb("wo", [P, 4, E])
        gam = sb("gam", [P, E])
        bet = sb("bet", [P, E])
        hT = sb("hT", [P, 2, 512])
        h_st = sb("h_st", [P, 2, 512])
        x_st = sb("x_st", [P, 2, 512])
        hb_tok = sb("hb_tok", [P, NT * E])
        x_tok = sb("x_tok", [P, NT * E])
        xT = sb("xT", [P, NT * E])
        stat = sb("stat", [P, 4, 6])
        mv = sb("mv", [P, 2, 4, 2])
        veps = sb("veps", [P, 2, 4])
        rstd = sb("rstd", [P, 2, 4])
        mhalf = sb("mhalf", [P, 4])
        xs = sb("xs", [P, 2, P])
        FT = sb("FT", [P, HEADS, 2, 2, P])
        comp = sb("comp", [P, 2, COMP])
        gmask = sb("gmask", [P, 2 * HEADS * 32])
        cc = sb("cc", [P, STEPS * COMP])
        rsum = sb("rsum", [P, STEPS, 2 * HEADS])
        beta = sb("beta", [P, STEPS, HEADS])
        bk = sb("bk", [P, STEPS, HEADS])
        gn = sb("gn", [P, STEPS * HEADS * STEPS])
        an = sb("an", [P, STEPS * HEADS * STEPS])
        inv = sb("inv", [P, STEPS * HEADS * STEPS])
        prod = sb("prod", [P, HEADS * STEPS * STEPS])
        nn = sb("nn", [P, STEPS * HEADS * STEPS])
        den = sb("den", [P, STEPS * HEADS])
        wc = sb("wc", [P, STEPS * HEADS * STEPS])
        wt = sb("wt", [P, 2, 2, HEADS * STEPS])
        wexp = X[:].rearrange("p u w -> p (u w)")[:, 0:4 * HEADS * P].rearrange("p (w u h t) -> p w u h t", w=2, u=2,
                                                                               h=HEADS)
        F_flat = F[:].rearrange("p u w -> p (u w)")
        vs = F_flat[:, 0:2048].rearrange("p (w u n) -> p w u n", w=2, u=2)
        oT = F_flat[:, 2048:4096].rearrange("p (w u c t) -> p w u c t", w=2, u=2, c=4)
        junk = F_flat[:, 4096:4096 + 12 * GE].rearrange("p (n e) -> p n e", e=GE)
        xa = sb("xa", [P, 2 * E])
        xn = sb("xn", [P, 2 * E])
        h2 = sb("h2", [P, 2, 2 * E])
        z = sb("z", [P, 2, 2 * E])
        fin = sb("fin", [P, 2, 2 * E])
        bits = sb("bits", [P, 2 * 64])
        top = sb("top", [P, 8])
        rem = sb("rem", [P, 8])
        U = sb("U", [P, 2, 2, GIN])
        UT = sb("UT", [GIN, 2, 2, P])
        w1s = sb("w1s", [GIN, 2, HID])
        w2s = sb("w2s", [P, HID])
        b2s = sb("b2s", [P, 3])
        opm = sb("opm", [P, 2, 2, 3])
        nop = sb("nop", [P, 2, 3])
        anyop = sb("anyop", [P, 2])
        act2 = sb("act2", [P, 2, 2])
        y = sb("y", [P, 12])
        res = sb("res", [P, 4])
        hot = sb("hot", [P, 64])
        comp_d = nc.dram_tensor("comp_scratch", (NT * P, COMP), F32, kind="Internal").ap()
        w_d = nc.dram_tensor("w_scratch", (NT * P, HEADS * STEPS), F32, kind="Internal").ap()

        pqk = ctx.enter_context(nc.psum_tensor("pqk", [P, 1024], F32))
        pv = ctx.enter_context(nc.psum_tensor("pv", [P, 512], F32))
        ptr = ctx.enter_context(nc.psum_tensor("ptr", [P, 2, 512], F32))
        pgr = ctx.enter_context(nc.psum_tensor("pgr", [P, 2, 512], F32))
        pms = ctx.enter_context(nc.psum_tensor("pms", [P, 512], F32))
        ident = cst[:, C_ID:C_ID + P]
        pback = [pms, pv]
        phid = [pqk[:], pgr[:].rearrange("p u n -> p (u n)")]

        s_cst, s_tau, s_wgt, s_spk, s_w = (sem(n) for n in (
            "consts_in", "taus_in", "latent_weights_in", "spikes_in", "weights_in"))
        s_trace = [sem("trace_in0"), sem("trace_in1")]
        s_exp = sem("latent_exp_done")
        s_lat = sem("latents_ready")
        s_dve = sem("vector_step")
        s_prod, s_pre = sem("pool_products"), sem("traces_decayed")
        s_anew, s_atr, s_aev = sem("attention_new"), sem("attention_transposed"), sem("attention_evacuated")
        s_hmm, s_hev, s_htr, s_htok = sem("h_product"), sem("h_evacuated"), sem("h_transposed"), sem("h_in_tokens")
        s_var, s_rstd, s_hb = sem("variance_ready"), sem("rstd_ready"), sem("h_plus_bias_ready")
        s_x, s_xtr, s_xT = sem("x_ready"), sem("x_transposed"), sem("xT_ready")
        s_xs, s_qk, s_v = sem("x_staged"), sem("qk_product"), sem("v_product")
        s_relu, s_vev = sem("relu_done"), sem("v_evacuated")
        s_f, s_ftr, s_fev = sem("features_ready"), sem("features_transposed"), sem("features_evacuated")
        s_gram, s_comp = sem("gram_ready"), sem("blocks_ready")
        s_cout = [sem("blocks_stored0"), sem("blocks_stored1")]
        s_cin, s_wc, s_wout = sem("blocks_loaded"), sem("mix_weights_solved"), sem("mix_weights_stored")
        s_bload = [sem("back_tiles_loaded0"), sem("back_tiles_loaded1")]
        s_wexp = sem("mix_weights_expanded")
        s_oT, s_oTs, s_y, s_xa = sem("out_product"), sem("out_evacuated"), sem("wo_product"), sem("residual_added")
        s_bvar, s_brstd = sem("back_variance"), sem("back_rstd")
        s_u, s_ut, s_uts = sem("mlp_in_ready"), sem("mlp_in_transposed"), sem("mlp_in_evacuated")
        s_hid, s_mlp = sem("hidden_ready"), sem("hidden_used")
        s_res, s_out = sem("result_ready"), [sem("result_stored0"), sem("result_stored1")]
        s_settled = sem("wait_carried")

        block = ctx.enter_context(nc.Block())

        def settled(eng):
            eng.sem_inc(s_settled, 1)

        @block.sync
        def _(sp):
            for credit_of, n in ((s_anew, 2), (s_atr, 2), (s_aev, 2), (s_hev, 2), (s_htr, 2), (s_htok, 2), (s_v, 2),
                                 (s_relu, 1), (s_vev, 1), (s_f, 32), (s_ftr, 16), (s_fev, 2), (s_comp, 2),
                                 (s_cout[0], 16), (s_cout[1], 16), (s_wc, 1), (s_wout, 16), (s_hb, 1), (s_xT, 1),
                                 (s_oT, 3), (s_y, 3), (s_oTs, 2), (s_wexp, 3), (s_xa, 2), (s_hid, 3), (s_ut, 2),
                                 (s_uts, 2), (s_mlp, 2), (s_out[0], 32), (s_out[1], 32)):
                sp.sem_inc(credit_of, n)
            sp.dma_start(lat[:, 2, :], tpre.rearrange("(f p) j -> p f j", p=P)).then_inc(s_tau, 16)
            sp.dma_start(lat[:, 3, :], tpost.rearrange("(f p) j -> p f j", p=P)).then_inc(s_tau, 16)
            sp.dma_start(lat[:, 0, :], wpre.rearrange("(f p) j -> p f j", p=P)).then_inc(s_wgt, 16)
            sp.dma_start(lat[:, 1, :], wpost.rearrange("(f p) j -> p f j", p=P)).then_inc(s_wgt, 16)
            with sp.Fori(0, HALVES) as hf:
                for k in range(CH):
                    sp.wait_ge(s_anew, hf * CH + k + 1)
                    settled(sp)
                    for n, src in enumerate((pre, post, att)):
                        sp.dma_start(trace[k % 2][n].rearrange("p (b j) -> p b j", b=SB),
                                     src[SB * k:SB * k + SB, bass.ds(hf * P, P), :].rearrange("b p j -> p b j")
                                     ).then_inc(s_trace[k % 2], 16)
            with sp.Fori(0, NT // 2) as m:
                t0 = m * 2
                for u in range(2):
                    sp.wait_ge(s_comp, t0 + (u + 1 + 2))
                    settled(sp)
                    sp.wait_ge(s_vev, t0 + (u + 1 + 1))
                    settled(sp)
                    sp.dma_start(comp_d[bass.ds((t0 + u) * P, P), :], comp[:, u, :]).then_inc(s_cout[u], 16)
            with sp.Fori(0, HALVES) as hf:
                for u in range(2):
                    sp.wait_ge(s_cout[u], hf * 64 + (64 + 16))
                    settled(sp)
                sp.wait_ge(s_wc, hf + 1)
                settled(sp)
                sp.dma_start(cc[:], comp_d[bass.ds(hf * (NT * P // 2), NT * P // 2), :].rearrange(
                    "(p s) c -> p (s c)", s=STEPS)).then_inc(s_cin, 16)
                sp.wait_ge(s_wc, hf + 2)
                settled(sp)
                sp.dma_start(w_d[bass.ds(hf * (NT * P // 2), NT * P // 2), :].rearrange(
                    "(p s) c -> p (s c)", s=STEPS), wc[:]).then_inc(s_wout, 16)
            sp.wait_ge(s_wout, 16 + 16 * HALVES)

            def load(p, w):
                sp.wait_ge(s_wexp, p * 2 + 1)
                settled(sp)
                sp.wait_ge(s_oT, p * 2 + 1)
                settled(sp)
                for u in range(2):
                    sp.dma_start(wt[:, w, u, :], w_d[bass.ds((p * 2 + u) * P, P), :]).then_inc(s_bload[w], 16)
                    sp.dma_start(vs[:, w, u, :], av(vst, (p * 2 + u) * 512, [1, 512])).then_inc(s_bload[w], 16)

            def store(p, w):
                sp.wait_ge(s_res, p + 1)
                settled(sp)
                for u in range(2):
                    sp.dma_start(out[:, bass.ds((p * 2 + u) * NPT, NPT), :].rearrange("t i e -> i t e"),
                                 fin[:, w, u * E:(u + 1) * E]).then_inc(s_out[w], 16)

            sp.wait_ge(s_f, 32 + 16 * NT)
            sp.wait_ge(s_ftr, 16 + 8 * NT)
            load(0, 0)
            load(1, 1)
            with sp.Fori(0, PAIRS // 2 - 1) as m:
                for w in range(2):
                    load(m * 2 + (w + 2), w)
                    store(m * 2 + w, w)
            store(PAIRS - 2, 0)
            store(PAIRS - 1, 1)
            for w in range(2):
                sp.wait_ge(s_out[w], 32 + 16 * PAIRS)

        @block.gpsimd
        def _(pool):
            pool.dma_start(spk_i, spk_rows.partition_broadcast(P)).then_inc(s_spk, 16)
            pool.dma_start(col_i[:], spk_cols.rearrange("(f p) b -> p f b", p=P)).then_inc(s_spk, 16)
            pool.dma_start(cst[:], consts).then_inc(s_cst, 16)
            pool.dma_start(vw[:], vwT.rearrange("(c p) e -> p c e", p=P)).then_inc(s_w, 16)
            pool.dma_start(vbias[:], vb).then_inc(s_w, 16)
            pool.dma_start(wqkv[:], wqkvT).then_inc(s_w, 16)
            pool.dma_start(wo[:], woT.rearrange("(c p) e -> p c e", p=P)).then_inc(s_w, 16)
            pool.dma_start(gam[:], lng.partition_broadcast(P)).then_inc(s_w, 16)
            pool.dma_start(bet[:], lnb.partition_broadcast(P)).then_inc(s_w, 16)
            pool.dma_start(w1s[:], w1.rearrange("r k n -> k r n")).then_inc(s_w, 16)
            pool.dma_start(w2s[:], w2.partition_broadcast(P)).then_inc(s_w, 16)
            pool.dma_start(b2s[:], b2.partition_broadcast(P)).then_inc(s_w, 16)
            pool.wait_ge(s_lat, 1)
            with pool.Fori(0, HALVES) as hf:
                for k in range(CH):
                    u = k % 2
                    c = hf * CH + k
                    pool.wait_ge(s_trace[u], hf * (48 * CH // 2) + 48 * (k // 2 + 1))
                    pool.wait_ge(s_anew, c + 1)
                    settled(pool)
                    nc.gpsimd.tensor_tensor(new_pre[u].rearrange("p (b j) -> p b j", b=SB),
                                            trace[u][0].rearrange("p (b j) -> p b j", b=SB),
                                            av(lat, hf * NEUR + 2 * 512, [0, SB], [1, NEUR]), ALU.mult)
                    nc.gpsimd.tensor_tensor(inc_pre[u].rearrange("p (b j) -> p b j", b=SB),
                                            av(spk_f, SB * k * NEUR, [NEUR, SB], [1, NEUR]),
                                            av(lat, hf * NEUR, [0, SB], [1, NEUR]), ALU.mult).then_inc(s_prod, 1)
                    pool.wait_ge(s_prod, c + 1)
                    nc.gpsimd.tensor_tensor(new_pre[u], new_pre[u], inc_pre[u], ALU.add)
                    nc.gpsimd.tensor_tensor(dec_post[u].rearrange("p (b j) -> p b j", b=SB),
                                            trace[u][1].rearrange("p (b j) -> p b j", b=SB),
                                            av(lat, hf * NEUR + 3 * 512, [0, SB], [1, NEUR]),
                                            ALU.mult).then_inc(s_pre, 1)
            pool.wait_ge(s_w, 16 * 9)
            with pool.Fori(0, 2) as m:
                g0 = m * 2
                for u in range(2):
                    pool.wait_ge(s_var, g0 + (u + 1))
                    nc.gpsimd.tensor_tensor(rstd[:, u, :], veps[:, u, :], mhalf[:], ALU.pow).then_inc(s_rstd, 1)
                    nc.gpsimd.tensor_tensor(av(hb_tok, (g0 + u) * 512, [E, 4], [1, E]),
                                            h_st[:, u, :].rearrange("p (t e) -> p t e", e=E),
                                            av(bet, 0, [0, 4], [1, E]), ALU.add).then_inc(s_hb, 1)

            def expand(p, w, u):
                if u == 0:
                    pool.wait_ge(s_bload[w], (p - w) * 32 + 64)
                    pool.wait_ge(s_oT, p * 2 + 1)
                nc.gpsimd.tensor_tensor(wexp[:, w, u].rearrange("p h (i t) -> p h i t", t=STEPS),
                                        av(wt, (2 * w + u) * 64, [STEPS, HEADS], [0, NPT], [1, STEPS]),
                                        av(cst, C_M16, [0, HEADS], [1, NPT], [0, STEPS]),
                                        ALU.mult).then_inc(s_wexp, 1)

            def power(p, n):
                pool.wait_ge(s_bvar, p * 2 + (n + 1))
                nc.gpsimd.tensor_tensor(rstd[:, n, 0:2], veps[:, n, 0:2], mhalf[:, 0:2], ALU.pow).then_inc(s_brstd, 1)

            def expand_and_power(p, w):
                for n in range(2):
                    expand(p + 1, 1 - w, n)
                    power(p, n)

            expand(0, 0, 0)
            expand(0, 0, 1)
            with pool.Fori(0, PAIRS // 2 - 1) as m:
                for w in range(2):
                    expand_and_power(m * 2 + w, w)
            expand_and_power(PAIRS - 2, 0)
            power(PAIRS - 1, 0)
            power(PAIRS - 1, 1)

        @block.scalar
        def _(act):
            act.wait_ge(s_tau, 32)
            nc.scalar.activation(lat[:, 2:4, :], lat[:, 2:4, :], ACT.Exp, scale=-1.0).then_inc(s_exp, 1)
            act.wait_ge(s_exp, 1)
            nc.scalar.activation(lat[:, 2:4, :], lat[:, 2:4, :], ACT.Exp, scale=-DT).then_inc(s_exp, 1)
            act.wait_ge(s_wgt, 32)
            nc.scalar.activation(lat[:, 0:2, :], lat[:, 0:2, :], ACT.Exp).then_inc(s_exp, 1)
            with act.Fori(0, HALVES) as hf:
                for k in range(CH):
                    act.wait_ge(s_atr, hf * CH + (k + 1 + 2))
                    for b in range(SB):
                        last = nc.scalar.activation(
                            av(attT, hf * (P * STEPS) + SB * k + b, [NEUR * STEPS, 2], [STEPS, P]),
                            ptr[:, k % 2, b * NEUR:(b + 1) * NEUR].rearrange("p (c i) -> p c i", c=2), ACT.Copy)
                    last.then_inc(s_aev, 1)
            act.wait_ge(s_w, 16 * 9)
            with act.Fori(0, 2) as m:
                g0 = m * 2
                for u in range(2):
                    g = g0 + u
                    act.wait_ge(s_hmm, g + 1)
                    act.wait_ge(s_htr, g + 1)
                    nc.scalar.activation(hT[:, u, :], pgr[:, u, :], ACT.Identity, bias=vbias[:]).then_inc(s_hev, 1)
                    act.wait_ge(s_x, g + 1)
                    nc.scalar.activation(av(x_tok, g * 512, [1, 512]), x_st[:, u, :], ACT.Copy)
                    act.wait_ge(s_xtr, g + 1)
                    nc.scalar.activation(av(xT, g * 512, [1, 512]), pqk[:, u * 512:(u + 1) * 512],
                                         ACT.Copy).then_inc(s_xT, 1)

            def stage(t, u):
                act.wait_ge(s_v, t + 1)
                nc.scalar.activation(xs[:, u, :], av(xT, t * P, [1, P]), ACT.Copy).then_inc(s_xs, 1)

            def evacuate_qkv(t, u):
                act.wait_ge(s_qk, t + 1)
                act.wait_ge(s_f, t * 16 + 16)
                xv = X[:, u, :].rearrange("p (j w) -> p j w", w=XW)
                qk = pqk[:].rearrange("p (j d) -> p j d", d=DH)
                nc.scalar.activation(xv[:, :, 2:2 + DH], qk, ACT.Relu)
                nc.scalar.activation(xv[:, :, 2 + DH:XW], qk, ACT.Relu, scale=-1.0)
                nc.scalar.activation(xv[:, :, 0:2], qk[:, :, DH - 2:DH], ACT.Relu, scale=-1.0).then_inc(s_relu, 1)
                act.wait_ge(s_v, t + (1 + 2))
                nc.scalar.activation(av(vst, t * 512, [1, 512]), pv[:], ACT.Copy)
                act.wait_ge(s_cout[u], (t - u) * 8 + 16)
                nc.scalar.activation(comp[:, u, OFF_BETA:COMP], pms[:, 0:HEADS], ACT.Exp,
                                     scale=-1.0).then_inc(s_vev, 1)

            def evacuate_features(t):
                for h in range(HEADS):
                    act.wait_ge(s_ftr, t * 8 + (16 + h + 1))
                    nc.scalar.activation(FT[:, h].rearrange("p r q t -> p (r q t)"), ptr[:, h % 2, :],
                                         ACT.Copy).then_inc(s_fev, 1)

            act.wait_ge(s_xT, 4 + 1)
            stage(0, 0)
            stage(1, 1)
            evacuate_qkv(0, 0)
            with act.Fori(0, NT // 2 - 1) as m:
                t0 = m * 2
                for u in range(2):
                    evacuate_qkv(t0 + (u + 1), 1 - u)
                    stage(t0 + (u + 2), u)
                    evacuate_features(t0 + u)
            evacuate_qkv(NT - 1, 1)
            evacuate_features(NT - 2)
            evacuate_features(NT - 1)


            def evacuate_out(p, w):
                for u in range(2):
                    act.wait_ge(s_oT, p * 2 + (u + 1 + 3))
                    act.wait_ge(s_y, p * 2 + 1)
                    nc.scalar.activation(oT[:, w, u].rearrange("p c t -> p (c t)"), ptr[:, u, :],
                                         ACT.Copy).then_inc(s_oTs, 1)

            def evacuate_mlp_in(p, w):
                act.wait_ge(s_ut, p + (1 + 2))
                act.wait_ge(s_hid, p * 2 + 1)
                nc.scalar.activation(UT[:, w].rearrange("k u t -> k (u t)"), pback[w][0:GIN, 2 * P:4 * P],
                                     ACT.Copy).then_inc(s_uts, 1)

            evacuate_out(0, 0)
            with act.Fori(0, PAIRS // 2 - 1) as m:
                for w in range(2):
                    evacuate_out(m * 2 + (w + 1), 1 - w)
                    evacuate_mlp_in(m * 2 + w, w)
            evacuate_out(PAIRS - 1, 1)
            evacuate_mlp_in(PAIRS - 2, 0)
            evacuate_mlp_in(PAIRS - 1, 1)

        @block.vector
        def _(dve):
            count = [0, 0]

            def link(ins):
                ins.then_inc(s_dve, 1)
                count[1] += 1
                dve.wait_ge(s_dve, count[0] + count[1])

            nc.vector.memset(mhalf[:], -0.5)
            nc.vector.memset(U[:], 1.0)
            nc.vector.memset(inv[:], 0.0)
            link(nc.vector.memset(nn[:], 0.0))
            nc.vector.memset(av(inv, 0, [65, STEPS], [8, HEADS]), 1.0)
            dve.wait_ge(s_spk, 32)
            nc.vector.tensor_copy(spk_f, spk_i)
            nc.vector.tensor_scalar(spk_m, spk_i, 0.0, None, ALU.not_equal)
            nc.vector.tensor_copy(col_f[:], col_i[:])
            nc.vector.tensor_scalar(col_m[:], col_i[:], 0.0, None, ALU.not_equal)
            dve.wait_ge(s_exp, 3)
            link(nc.vector.tensor_scalar(lat[:, 0:2, :], lat[:, 0:2, :], DT, None, ALU.mult))
            nc.vector.memset(rstd[:], 0.0).then_inc(s_lat, 1)
            before = count[1]
            with dve.Fori(0, HALVES) as hf:
                for k in range(CH):
                    count[0] = hf * (6 * CH)
                    u = k % 2
                    c = hf * CH + k
                    dve.wait_ge(s_trace[u], hf * (48 * CH // 2) + 48 * (k // 2 + 1))
                    dve.wait_ge(s_pre, c + 1)

                    def halves(out_, in0, col, in1, in0_fixed=None):
                        for b in range(SB):
                            js = slice(b * NEUR, (b + 1) * NEUR)
                            last = nc.vector.scalar_tensor_tensor(
                                out_[:, js], in0_fixed if in0_fixed is not None else in0[:, js],
                                av(col, hf * STEPS + SB * k + b, [1, 1]), in1[:, js], ALU.mult, ALU.add)
                        return last

                    np_, dp, atn = new_pre[u], dec_post[u], trace[u][2]
                    link(halves(new_post, None, col_f, dp, av(lat, hf * NEUR + 512, [1, NEUR])))
                    link(nc.vector.tensor_tensor(mix, new_post, spk_m[:, SB * k * NEUR:SB * (k + 1) * NEUR],
                                                 ALU.mult))
                    link(halves(mix, np_, col_m, mix))
                    link(nc.vector.tensor_tensor(new_post, atn, mix, ALU.mult))
                    link(nc.vector.tensor_tensor(new_post, atn, new_post, ALU.subtract))
                    dve.wait_ge(s_atr, c + 1)
                    link(halves(anew[u], np_, col_m, new_post))
                    nc.vector.tensor_scalar(anew[u], anew[u], -0.5, 1.5, ALU.max,
                                            ALU.min).then_inc(s_anew, 1)
            assert count[1] - before == 6 * CH
            count[:] = [0, before + 6 * CH * HALVES]

            before = count[1]
            with dve.Fori(0, 2) as m:
                g0 = m * 2
                for u in range(2):
                    count[0] = g0
                    g = g0 + u
                    dve.wait_ge(s_htr, g + (1 + 2))
                    dve.wait_ge(s_hb, g0 + 1)
                    nc.vector.tensor_copy(h_st[:, u, :], ptr[:, u, :])
                    for t in range(4):
                        last = nc.vector.bn_stats(stat[:, t, :], ptr[:, u, t * E:(t + 1) * E])
                    last.then_inc(s_htok, 1)
                    dve.wait_ge(s_htok, g + (1 + 2))
                    settled(dve)
                    for t in range(4):
                        last = nc.vector.bn_aggr(mv[:, u, t, :], stat[:, t, :])
                    link(last)
                    nc.vector.tensor_scalar(veps[:, u, :], mv[:, u, :, 1], EPS, None, ALU.add).then_inc(s_var, 1)
                    dve.wait_ge(s_rstd, g + 1)
                    dve.wait_ge(s_xT, g0 + 1)
                    for t in range(4):
                        last = nc.vector.tensor_scalar(x_st[:, u, t * E:(t + 1) * E], h_st[:, u, t * E:(t + 1) * E],
                                                       mv[:, u, t, 0:1], rstd[:, u, t:t + 1], ALU.subtract, ALU.mult)
                    last.then_inc(s_x, 1)
            assert count[1] - before == 2
            count[:] = [0, before + 4]

            def features(t, u):
                dve.wait_ge(s_relu, t + (1 + 1))
                dve.wait_ge(s_ftr, t * 8 + 8)
                dve.wait_ge(s_cout[u], (t - u) * 8 + 16)
                for j in range(2 * HEADS):
                    base = u * 2 * HEADS * XW + j * XW
                    nc.vector.scalar_tensor_tensor(
                        F[:, u, j * FEAT:(j + 1) * FEAT].rearrange("p (r d) -> p r d", r=2),
                        av(X, base + 2, [0, 2], [1, 2 * DH]), 1.0, av(X, base, [1, 2], [1, 2 * DH]),
                        ALU.mult, ALU.mult,
                        accum_out=comp[:, u, OFF_SUM + j:OFF_SUM + j + 1]).then_inc(s_f, 1)

            def blocks(t, u):
                dve.wait_ge(s_comp, t + 2)
                dve.wait_ge(s_gram, t + 1)
                link(nc.vector.tensor_tensor(gmask[:].rearrange("p (j i t) -> p j i t", i=QW, t=STEPS),
                                             pgr[:, u, :].rearrange("p (j i t) -> p j i t", i=QW, t=STEPS),
                                             av(cst, C_M4, [0, 2 * HEADS], [1, QW], [0, STEPS]), ALU.mult))
                nc.vector.tensor_reduce(comp[:, u, 0:OFF_SUM].rearrange("p (j t) -> p j t", t=STEPS),
                                        av(gmask, 0, [32, 2 * HEADS], [1, STEPS], [STEPS, QW]), AX_X,
                                        ALU.add).then_inc(s_comp, 1)

            features(0, 0)
            before = count[1]
            with dve.Fori(0, NT // 2 - 1) as m:
                t0 = m * 2
                for u in range(2):
                    count[0] = t0
                    features(t0 + (u + 1), 1 - u)
                    blocks(t0 + u, u)
            assert count[1] - before == 2
            count[:] = [0, before + NT - 2]
            features(NT - 1, 1)
            blocks(NT - 2, 0)
            blocks(NT - 1, 1)

            T3 = STEPS * HEADS
            before = count[1]
            with dve.Fori(0, HALVES) as hf:
                count[0] = hf * SOLVE_LINKS
                dve.wait_ge(s_cin, hf * 16 + 16)
                ccv = cc[:].rearrange("p (s c) -> p s c", c=COMP)
                nc.vector.reciprocal(rsum[:], ccv[:, :, OFF_SUM:OFF_BETA])
                link(nc.vector.tensor_scalar(beta[:], ccv[:, :, OFF_BETA:COMP], 1.0, None, ALU.add))
                link(nc.vector.reciprocal(beta[:], beta[:]))
                rk = av(rsum, 0, [0, STEPS], [2, HEADS], [2 * HEADS, STEPS])
                link(nc.vector.tensor_tensor(bk[:], beta[:], av(rsum, 0, [2 * HEADS, STEPS], [2, HEADS]), ALU.mult))
                d3 = dict(t=STEPS, h=HEADS)
                gv = gn[:].rearrange("p (t h s) -> p t h s", **d3)
                an_v = an[:].rearrange("p (t h s) -> p t h s", **d3)
                nc.vector.tensor_tensor(gv, av(cc, 0, [1, STEPS], [16, HEADS], [COMP, STEPS]), rk, ALU.mult)
                link(nc.vector.tensor_tensor(an_v, av(cc, 8, [1, STEPS], [16, HEADS], [COMP, STEPS]), rk, ALU.mult))
                nc.vector.tensor_tensor(gv, gv, av(bk, 0, [HEADS, STEPS], [1, HEADS], [0, STEPS]), ALU.mult)
                link(nc.vector.tensor_tensor(an_v, an_v, av(rsum, 1, [2 * HEADS, STEPS], [2, HEADS], [0, STEPS]),
                                             ALU.mult))
                link(nc.vector.tensor_tensor(an_v, an_v, av(cst, C_CAUS, [STEPS, STEPS], [0, HEADS], [1, STEPS]),
                                             ALU.mult))
                link(nc.vector.tensor_reduce(den[:], an[:].rearrange("p (a s) -> p a s", s=STEPS), AX_X, ALU.add))
                link(nc.vector.tensor_scalar(den[:], den[:], EPS, None, ALU.add))
                link(nc.vector.reciprocal(den[:], den[:]))
                link(nc.vector.tensor_scalar(den[:], den[:], float(DH) ** -0.5, None, ALU.mult))

                def row(dst, coef, t, n, negate):
                    pr_ = av(prod, 0, [n * n, HEADS], [n, n], [1, n])
                    link(nc.vector.tensor_tensor(pr_, av(inv, 0, [8, HEADS], [1, n], [T3, n]),
                                                 av(coef, t * T3, [8, HEADS], [0, n], [1, n]), ALU.mult))
                    link(nc.vector.tensor_reduce(av(dst, t * T3, [8, HEADS], [1, n]), pr_, AX_X, ALU.add,
                                                 negate=negate))

                for t in range(1, STEPS):
                    row(inv, gn, t, t, True)
                for t in range(STEPS):
                    row(nn, an, t, t + 1, False)
                dve.wait_ge(s_wout, hf * 16 + 16)
                link(nc.vector.tensor_tensor(nn[:].rearrange("p (a u) -> p a u", u=STEPS),
                                             nn[:].rearrange("p (a u) -> p a u", u=STEPS),
                                             av(den, 0, [1, STEPS * HEADS], [0, STEPS]), ALU.mult))
                nc.vector.tensor_tensor(wc[:].rearrange("p (u h t) -> p u h t", u=STEPS, h=HEADS),
                                        av(nn, 0, [1, STEPS], [8, HEADS], [T3, STEPS]),
                                        av(beta, 0, [HEADS, STEPS], [1, HEADS], [0, STEPS]),
                                        ALU.mult).then_inc(s_wc, 1)
            assert count[1] - before == SOLVE_LINKS, count[1] - before
            count[:] = [0, before + SOLVE_LINKS * HALVES]

            def w2v(t):
                return t.rearrange("p (u e) -> p u e", u=2)

            def stats(src, n):
                for u in range(2):
                    last = nc.vector.bn_stats(stat[:, u, :], src[:, u * E:(u + 1) * E])
                link(last)
                settled(dve)
                for u in range(2):
                    last = nc.vector.bn_aggr(mv[:, n, u, :], stat[:, u, :])
                link(last)
                nc.vector.tensor_scalar(veps[:, n, 0:2], mv[:, n, 0:2, 1], EPS, None, ALU.add).then_inc(s_bvar, 1)

            def normalise(src, dst, p, n):
                dve.wait_ge(s_brstd, p * 2 + (n + 1))
                for u in range(2):
                    last = nc.vector.tensor_scalar(dst[:, u * E:(u + 1) * E], src[:, u * E:(u + 1) * E],
                                                   mv[:, n, u, 0:1], rstd[:, n, u:u + 1], ALU.subtract, ALU.mult)
                link(last)

            def residual(p, w):
                dve.wait_ge(s_y, p * 2 + (2 + 3))
                nc.vector.tensor_tensor(xa[:], av(x_tok, p * 2 * E, [1, 2 * E]), pback[w][:, 0:2 * E],
                                        ALU.add).then_inc(s_xa, 1)
                dve.wait_ge(s_xa, p + (1 + 2))
                stats(xa, 0)

            def second_norm(p, w):
                normalise(xa, xn, p, 0)
                link(nc.vector.tensor_tensor(w2v(xn[:]), w2v(xn[:]), av(gam, 0, [0, 2], [1, E]), ALU.mult))
                link(nc.vector.tensor_tensor(h2[:, w], xn[:], av(hb_tok, p * 2 * E, [1, 2 * E]), ALU.add))
                stats(h2[:, w], 1)

            def mlp_inputs(p, w):
                normalise(h2[:, w], z[:, w], p, 1)
                zw = w * 2 * E
                link(nc.vector.scalar_tensor_tensor(w2v(bits[:]), av(z, zw + 16, [E, 2], [1, 64]), 0.5,
                                                    av(cst, C_RAMP, [0, 2], [1, 64]), ALU.is_gt, ALU.mult))
                link(nc.vector.tensor_reduce(top[:], bits[:].rearrange("p (n b) -> p n b", b=16), AX_X, ALU.max))
                link(nc.vector.tensor_scalar(rem[:], top[:], -1.0, 16.0, ALU.mult, ALU.add))
                dve.wait_ge(s_ut, p + 1)
                nc.vector.scalar_tensor_tensor(U[:, w, :, 0:4], top[:].rearrange("p (u n) -> p u n", u=2), 0.0,
                                               rem[:].rearrange("p (u n) -> p u n", u=2), ALU.is_gt, ALU.mult)
                nc.vector.tensor_copy(U[:, w, :, 4:7], av(z, zw + 1, [E, 2], [1, 3])).then_inc(s_u, 1)
                om = opm[:, w]
                link(nc.vector.tensor_scalar(om, av(z, zw + 1, [E, 2], [1, 3]), 0.5, None, ALU.is_gt))
                nc.vector.tensor_reduce(anyop[:], om, AX_X, ALU.max)
                link(nc.vector.tensor_scalar(nop[:], om, -1.0, 1.0, ALU.mult, ALU.add))
                nc.vector.tensor_tensor(om[:, :, 1], om[:, :, 1], nop[:, :, 0], ALU.mult)
                nc.vector.tensor_tensor(om[:, :, 2], nop[:, :, 0], nop[:, :, 1], ALU.mult)
                link(nc.vector.tensor_scalar(act2[:, w], av(z, zw, [E, 2]), 0.5, 2.0, ALU.is_ge, ALU.mult))
                link(nc.vector.tensor_tensor(act2[:, w], act2[:, w], anyop[:], ALU.mult))

            def second_layer(p, u):
                dve.wait_ge(s_hid, p * 2 + (u + 1 + 3))
                for r in range(2):
                    for op in range(3):
                        last = nc.vector.scalar_tensor_tensor(
                            junk[:, u * 6 + r * 3 + op, :], phid[u][:, r * 512 + op * GE:r * 512 + (op + 1) * GE], 0.0,
                            w2s[:, op * GE:(op + 1) * GE], ALU.max, ALU.mult,
                            accum_out=y[:, u * 6 + r * 3 + op:u * 6 + r * 3 + op + 1])
                last.then_inc(s_mlp, 1)

            def finish(p, w):
                zw = w * 2 * E
                dve.wait_ge(s_mlp, p * 2 + (2 + 2))
                link(nc.vector.tensor_tensor(y[:].rearrange("p (a o) -> p a o", o=3),
                                             y[:].rearrange("p (a o) -> p a o", o=3),
                                             av(b2s, 0, [0, 4], [1, 3]), ALU.add))
                link(nc.vector.tensor_tensor(y[:].rearrange("p (u r o) -> p u r o", r=2, o=3),
                                             y[:].rearrange("p (u r o) -> p u r o", r=2, o=3),
                                             av(opm, w * 6, [3, 2], [0, 2], [1, 3]), ALU.mult))
                link(nc.vector.tensor_reduce(res[:], y[:].rearrange("p (a o) -> p a o", o=3), AX_X, ALU.add))
                link(nc.vector.tensor_scalar(res[:], res[:], -1.0, 16.0, ALU.max, ALU.min))
                link(nc.vector.tensor_scalar(res[:], res[:], ROUND, ROUND, ALU.add, ALU.subtract))
                link(nc.vector.tensor_scalar(res[:], res[:], 0.0, 15.0, ALU.max, ALU.min))
                link(nc.vector.tensor_tensor(hot[:].rearrange("p (a k) -> p a k", k=16),
                                             av(cst, C_IOTA, [0, 4], [1, 16]), av(res, 0, [1, 4], [0, 16]),
                                             ALU.is_equal))
                link(nc.vector.tensor_tensor(w2v(hot[:]), w2v(hot[:]), av(act2, w * 2, [1, 2], [0, 32]), ALU.mult))
                zo = av(z, zw + 80, [E, 2], [1, 32])
                link(nc.vector.tensor_tensor(zo, zo, w2v(hot[:]), ALU.add))
                dve.wait_ge(s_out[w], (p - w) * 16 + 32)
                nc.vector.tensor_tensor(fin[:, w], h2[:, w], z[:, w], ALU.add).then_inc(s_res, 1)

            def back_and_finish(p, w):
                residual(p, w)
                second_layer(p - 1, 0)
                second_norm(p, w)
                second_layer(p - 1, 1)
                mlp_inputs(p, w)
                finish(p - 1, 1 - w)

            residual(0, 0)
            second_norm(0, 0)
            mlp_inputs(0, 0)
            before = count[1]
            with dve.Fori(0, PAIRS // 2 - 1) as m:
                count[0] = m * (2 * BACK_LINKS)
                for w in range(2):
                    back_and_finish(m * 2 + (w + 1), 1 - w)
            assert count[1] - before == 2 * BACK_LINKS, count[1] - before
            count[:] = [0, before + (PAIRS - 2) * BACK_LINKS]
            back_and_finish(PAIRS - 1, 1)
            for u in range(2):
                second_layer(PAIRS - 1, u)
            finish(PAIRS - 1, 1)

        @block.tensor
        def _(pe):
            mm, tr = nc.tensor.matmul, nc.tensor.transpose
            pe.wait_ge(s_cst, 16)
            with pe.Fori(0, HALVES) as hf:
                for k in range(CH):
                    c = hf * CH + k
                    pe.wait_ge(s_anew, c + (1 + 2))
                    pe.wait_ge(s_aev, c + 1)
                    for n in range(4):
                        last = tr(ptr[:, k % 2, n * P:(n + 1) * P], anew[k % 2][:, n * P:(n + 1) * P], ident)
                    last.then_inc(s_atr, 1)
            pe.wait_ge(s_aev, HALVES * CH + 2)
            pe.wait_ge(s_w, 16 * 9)
            with pe.Fori(0, 2) as m:
                g0 = m * 2
                for u in range(2):
                    g = g0 + u
                    pe.wait_ge(s_hev, g + 1)
                    for c in range(2):
                        last = mm(pgr[:, u, :], vw[:, c, :], av(attT, g * 512 + c * NEUR * STEPS, [1, 512]),
                                  start=(c == 0), stop=(c == 1))
                    last.then_inc(s_hmm, 1)
                    pe.wait_ge(s_hev, g + (1 + 2))
                    pe.wait_ge(s_htok, g + 1)
                    for t in range(4):
                        last = tr(ptr[:, u, t * P:(t + 1) * P], hT[:, u, t * P:(t + 1) * P], ident)
                    last.then_inc(s_htr, 1)
                    pe.wait_ge(s_x, g + 1)
                    pe.wait_ge(s_xT, g0 + 1)
                    for t in range(4):
                        last = tr(pqk[:, u * 512 + t * P:u * 512 + (t + 1) * P], x_st[:, u, t * P:(t + 1) * P], ident)
                    last.then_inc(s_xtr, 1)

            def project(t, u):
                pe.wait_ge(s_xs, t + 1)
                pe.wait_ge(s_relu, t + 1)
                for n in range(2):
                    last = mm(pqk[:, n * 512:(n + 1) * 512], xs[:, u, :], wqkv[:, n * 512:(n + 1) * 512],
                              start=True, stop=True)
                last.then_inc(s_qk, 1)
                pe.wait_ge(s_vev, t + 1)
                mm(pv[:], xs[:, u, :], wqkv[:, 1024:1536], start=True, stop=True)
                mm(pms[:, 0:HEADS], xs[:, u, :], wqkv[:, 1536:1544], start=True, stop=True).then_inc(s_v, 1)

            def gram(t, u, h):
                pe.wait_ge(s_fev, t * 8 + (h + 1 + 2))
                if h == 0:
                    pe.wait_ge(s_comp, t + 1)
                for g in range(NQ):
                    for r in range(2):
                        last = mm(pgr[32 * g:32 * g + 32, u, h * 64:(h + 1) * 64], FT[:, h, r, 0, 32 * g:32 * g + 32],
                                  av(FT, h * 512 + r * 256 + 32 * g, [P, 2], [1, 32]), start=(r == 0), stop=(r == 1))
                if h == HEADS - 1:
                    last.then_inc(s_gram, 1)

            def transpose_and_multiply(t, u):
                for h in range(HEADS):
                    pe.wait_ge(s_f, t * 16 + (32 + 2 * h + 2))
                    pe.wait_ge(s_fev, t * 8 + (h + 1))
                    for r in range(2):
                        for q in range(2):
                            src = (2 * h + q) * FEAT + r * 2 * DH
                            last = tr(ptr[:, h % 2, (2 * r + q) * P:(2 * r + q + 1) * P], F[:, u, src:src + P], ident)
                    last.then_inc(s_ftr, 1)
                    if h:
                        gram(t, u, h - 1)
                gram(t, u, HEADS - 1)

            project(0, 0)
            with pe.Fori(0, NT // 2 - 1) as m:
                t0 = m * 2
                for u in range(2):
                    project(t0 + (u + 1), 1 - u)
                    transpose_and_multiply(t0 + u, u)
            project(NT - 1, 1)
            transpose_and_multiply(NT - 2, 0)
            transpose_and_multiply(NT - 1, 1)


            def mix_values(p, w):
                for u in range(2):
                    pe.wait_ge(s_wexp, p * 2 + (u + 1 + 3))
                    pe.wait_ge(s_oTs, p * 2 + (u + 1))
                    for h in range(HEADS):
                        p0 = DH * (h % 2)
                        last = mm(ptr[p0:p0 + DH, u, (h // 2) * P:(h // 2 + 1) * P],
                                  vs[:, w, u, h * DH:(h + 1) * DH], wexp[:, w, u, h, :], start=True, stop=True)
                    last.then_inc(s_oT, 1)
                pe.wait_ge(s_xa, p + 1)
                pe.wait_ge(s_uts, p + 1)
                for u in range(2):
                    pe.wait_ge(s_oTs, p * 2 + (u + 1 + 2))
                    for c in range(4):
                        last = mm(pback[w][:, u * P:(u + 1) * P], oT[:, w, u, c, :], wo[:, c, :], start=(c == 0),
                                  stop=(c == 3))
                    last.then_inc(s_y, 1)

            def first_layer(p, w):
                pe.wait_ge(s_u, p + 1)
                for u in range(2):
                    last = mm(pback[w][0:GIN, (2 + u) * P:(3 + u) * P], U[:, w, u, :], ident, start=True, stop=True)
                last.then_inc(s_ut, 1)
                pe.wait_ge(s_uts, p + (1 + 2))
                for u in range(2):
                    pe.wait_ge(s_mlp, p * 2 + (u + 1))
                    for r in range(2):
                        last = mm(phid[u][:, r * 512:r * 512 + HID], UT[:, w, u, :], w1s[:, r, :], start=True, stop=True)
                    last.then_inc(s_hid, 1)

            mix_values(0, 0)
            with pe.Fori(0, PAIRS // 2 - 1) as m:
                for w in range(2):
                    mix_values(m * 2 + (w + 1), 1 - w)
                    first_layer(m * 2 + w, w)
            mix_values(PAIRS - 1, 1)
            first_layer(PAIRS - 2, 0)
            first_layer(PAIRS - 1, 1)


def constants():
    c = np.zeros((P, C_ALL), np.float32)
    p = np.arange(P)
    c[p, C_ID + p] = 1
    c[p, C_M16 + p // STEPS] = 1
    c[p, C_M4 + p % 32 // STEPS] = 1
    t = np.arange(STEPS)
    c[:, C_CAUS:C_CAUS + 64] = (t[None, :] <= t[:, None]).astype(np.float32).reshape(-1)
    c[:, C_RAMP:C_RAMP + 64] = np.tile(16 - np.arange(16), 4)
    c[:, C_IOTA:C_IOTA + 16] = np.arange(16)
    return c


def kernel(**inputs):
    import concourse.bacc as bacc
    from concourse.bass_utils import run_bass_kernel_spmd

    a = {k: np.asarray(v) for k, v in inputs.items()}
    ffn = {op: {n: a[f"L0_ffn_{op}_{n}"] for n in ("w1", "b1", "w2", "b2")} for op in ("and", "or", "xor")}
    wh = a["L0_attn_W_qkvb"].reshape(HEADS, 3 * DH + 1, E)
    wqkv = np.concatenate([np.concatenate([wh[:, DH:2 * DH], wh[:, 0:DH]], 1).reshape(-1, E),
                           wh[:, 2 * DH:3 * DH].reshape(-1, E), wh[:, 3 * DH]], 0).T
    w1 = np.zeros((2, GIN, HID), np.float32)
    for n, op in enumerate(ffn.values()):
        cols = slice(n * GE, (n + 1) * GE)
        for r in range(2):
            w1[r, r, cols], w1[r, 2 + r, cols] = op["w1"][0], op["w1"][1]
            w1[r, 4, cols], w1[r, 5, cols], w1[r, 6, cols] = op["w1"][46], op["w1"][44], op["w1"][45]
            w1[r, 7, cols] = op["b1"]
    arrays = {
        "spk_rows": a["x"].reshape(-1), "spk_cols": a["x"].T,
        "pre": a["fside_BSS_pre_trace"], "post": a["fside_BSS_post_trace"], "att": a["fside_BSS_attention"],
        "wpre": a["L0_tok_latent_pre_weight"][0], "wpost": a["L0_tok_latent_post_weight"][0],
        "tpre": a["L0_tok_latent_pre_tau_s"][0], "tpost": a["L0_tok_latent_post_tau_s"][0],
        "vwT": a["L0_tok_v_w"].T, "vb": a["L0_tok_v_b"].reshape(E, 1), "wqkvT": wqkv, "woT": a["L0_attn_W_o"].T,
        "lng": a["L0_attn_ln_g"], "lnb": a["L0_attn_ln_b"], "w1": w1,
        "w2": np.concatenate([op["w2"][:, 64] for op in ffn.values()]),
        "b2": np.concatenate([op["b2"][64:65] for op in ffn.values()]), "consts": constants(),
    }
    arrays = {k: np.ascontiguousarray(v) for k, v in arrays.items()}
    nc = bacc.Bacc("TRN2", target_bir_lowering=False, num_devices=1)
    args = [nc.dram_tensor(k, v.shape, mybir.dt.from_np(v.dtype), kind="ExternalInput").ap()
            for k, v in arrays.items()]
    out = nc.dram_tensor("out", (STEPS, NEUR, E), F32, kind="ExternalOutput").ap()
    build(nc, *args, out)
    return run_bass_kernel_spmd(nc, [arrays], core_ids=[0]).results[0]["out"]
```

```python
from contextlib import ExitStack

import numpy as np

import concourse.bass as bass
from concourse import mybir

F32 = mybir.dt.float32
BF16 = mybir.dt.bfloat16
I32 = mybir.dt.int32
ALU = mybir.AluOpType
ACT = mybir.ActivationFunctionType
AX_X = mybir.AxisListType.X

P = 128
STEPS = 8
NEUR = 256
E = 128
HEADS, DH = 8, 64
NT = STEPS * NEUR // P
NPT = P // STEPS
HALVES = NEUR // P
SB = 2
CH = STEPS // SB
FEAT = 2 * 2 * DH
XW = 2 * DH + 2
QW = 4
NQ = P // 32
COMP = 2 * HEADS * STEPS + 3 * HEADS
OFF_SUM, OFF_BETA = 2 * HEADS * STEPS, 2 * HEADS * STEPS + 2 * HEADS
GE = 160
SPLIT = 3
FLAG0 = 5 * SPLIT
ROWS = FLAG0 + 3 * SPLIT * SPLIT
OPS = 3
GIN = OPS * ROWS
HC = GE + 1
DT = 0.001
EPS = 1e-5
ROUND = 12582912.0
C_ID, C_M16, C_M4, C_CAUS, C_RAMP, C_IOTA, C_PART = 0, 128, 144, 148, 212, 276, 292
C_ALL = 294
PAIRS = NT // 2
GROUPS = NT // 4
DVE_ADDS = (0, 2)
TWO_PAIRS = 50


def av(t, off, *dims, parts=P, p0=0):
    a = t[:]
    step = a.ap[0][0]
    return bass.AP(a.tensor, a.offset + p0 * step + off, [[step, parts]] + [list(d) for d in dims])


def build(nc, spk_rows, spk_cols, pre, post, att, wpre, wpost, tpre, tpost, vwT, vb, wqkvT, woT, lng, lnb,
          w1, consts, out):
    ctx = ExitStack()
    with ctx:
        def sb(name, shape, dt=F32):
            return ctx.enter_context(nc.sbuf_tensor(name, shape, dt))

        def sem(name):
            return ctx.enter_context(nc.semaphore(name))

        cst = sb("cst", [P, C_ALL])
        X = sb("X", [P, 2, 2 * HEADS * XW])
        spk_i = X[:, 0, 0:STEPS * NEUR].bitcast(I32)
        attT = sb("attT", [P, 2 * NEUR * STEPS])
        spk_f = sb("spk_f", [P, NEUR * STEPS])[:]
        spk_m = sb("spk_m", [P, NEUR * STEPS])[:]
        col_i = sb("col_i", [P, HALVES * STEPS], I32)
        col_f = sb("col_f", [P, HALVES * STEPS])
        col_m = sb("col_m", [P, HALVES * STEPS])
        lat = sb("lat", [P, 4, HALVES * NEUR])
        F = sb("F", [P, 2, 2 * HEADS * FEAT])
        FT = sb("FT", [P, HEADS, 2, 2, P])
        FT_flat = FT[:].rearrange("p h r q t -> p (h r q t)")
        parts = iter([t[:, n * SB * NEUR:(n + 1) * SB * NEUR] for t, count in (
            (F[:].rearrange("p u w -> p (u w)"), 16), (FT_flat, 8)) for n in range(count)])
        trace = [[next(parts) for _ in range(3)] for _ in range(CH)]
        inc_pre, dec_post, new_pre, anew = ([next(parts), next(parts)] for _ in range(4))
        new_post, mix = next(parts), next(parts)
        vw = sb("vw", [P, 2, E])
        vbias = sb("vbias", [P, 1])
        wqkv = sb("wqkv", [P, HEADS * (3 * DH + 1)])
        wo = sb("wo", [P, 4, E])
        gam = sb("gam", [P, E])
        bet = sb("bet", [P, E])
        hT = sb("hT", [P, 2, 512])
        h_st = sb("h_st", [P, 2, 512])
        x_st = sb("x_st", [P, 2, 512])
        hb_tok = sb("hb_tok", [P, NT * E])
        x_tok = sb("x_tok", [P, NT * E])
        xT = sb("xT", [P, NT * E])
        stat = sb("stat", [P, 4, 6])
        mv = sb("mv", [P, 2, 4, 2])
        veps = sb("veps", [P, 2, 4])
        rstd = sb("rstd", [P, 2, 4])
        mhalf = sb("mhalf", [P, 4])
        xs = sb("xs", [P, 2, P])
        comp = sb("comp", [P, 2, COMP])
        gmask = sb("gmask", [P, 2 * HEADS * 32])
        cc = sb("cc", [P, STEPS * COMP])
        rsum = sb("rsum", [P, STEPS, 2 * HEADS])
        beta = sb("beta", [P, STEPS, HEADS])
        bk = sb("bk", [P, STEPS, HEADS])
        gn = sb("gn", [P, STEPS * HEADS * STEPS])
        an = sb("an", [P, STEPS * HEADS * STEPS])
        inv = sb("inv", [P, STEPS * HEADS * STEPS])
        prod = sb("prod", [P, 2, HEADS * STEPS * STEPS])
        nn = sb("nn", [P, STEPS * HEADS * STEPS])
        den = sb("den", [P, STEPS * HEADS])
        wc = sb("wc", [P, STEPS * HEADS * STEPS])
        xv = sb("xv", [P, 2, 2, P])
        wt = sb("wt", [P, 2, 2, HEADS * STEPS])
        wexp = attT[:].rearrange("p (w u h t) -> p w u h t", w=2, u=2, h=HEADS)
        F_flat = F[:].rearrange("p u w -> p (u w)")
        vs = F_flat[:, 0:2048].rearrange("p (w u n) -> p w u n", w=2, u=2)
        oT = F_flat[:, 2048:4096].rearrange("p (w u c t) -> p w u c t", w=2, u=2, c=4)
        junk = F_flat[:, 4096:4096 + 4 * HC].rearrange("p (n e) -> p n e", e=HC)
        z_all = FT_flat[:, 0:NT * E]
        h2_all = FT_flat[:, NT * E:2 * NT * E]
        xa = sb("xa", [P, 2 * E])
        xn = sb("xn", [P, 2 * E])
        bits = sb("bits", [P, 2 * 64])
        top = sb("top", [P, 8])
        rem = sb("rem", [P, 8])
        nib = sb("nib", [P, 2, 4])
        flag = sb("flag", [P, 2, 3])
        Ub = sb("Ub", [P, 2, ROWS], BF16)
        om = sb("om", [P, 2, OPS])
        no = sb("no", [P, 2, OPS])
        U = sb("U", [P, 2, 2, OPS, ROWS], BF16)
        UT = sb("UT", [GIN, 2, 2, P], BF16)
        ident_b = sb("ident_b", [P, P], BF16)
        w2c = sb("w2c", [P, 2, HC])
        w1b = sb("w1b", [GIN, 3 * HC], BF16)
        w1s = sb("w1s", [GIN, 3 * HC])
        opm = sb("opm", [P, 4, 3])
        anyop = sb("anyop", [P, 4])
        act2 = sb("act2", [P, 4])
        y = sb("y", [P, 8])
        res = sb("res", [P, 8])
        hot = sb("hot", [P, 8 * 16])
        comp_d = nc.dram_tensor("comp_scratch", (NT * P, COMP), F32, kind="Internal").ap()
        w_d = nc.dram_tensor("w_scratch", (NT * P, HEADS * STEPS), F32, kind="Internal").ap()

        pqk = ctx.enter_context(nc.psum_tensor("pqk", [P, 1024], F32))
        pv = ctx.enter_context(nc.psum_tensor("pv", [P, 512], F32))
        ptr = ctx.enter_context(nc.psum_tensor("ptr", [P, 2, 512], F32))
        pgr = ctx.enter_context(nc.psum_tensor("pgr", [P, 2, 512], F32))
        pms = ctx.enter_context(nc.psum_tensor("pms", [P, 512], F32))
        ident = cst[:, C_ID:C_ID + P]
        pback = [pms, pv]
        phid = [pqk[:, 0:512], pqk[:, 512:1024]]

        s_cst, s_tau, s_wgt, s_spk, s_w = (sem(n) for n in (
            "consts_in", "taus_in", "latent_weights_in", "spikes_in", "weights_in"))
        s_trace = [sem(f"trace_in{k}") for k in range(CH)]
        s_exp = sem("latent_exp_done")
        s_lat = sem("latents_ready")
        s_dve = sem("vector_step")
        s_prod, s_pre, s_dpost = sem("pool_products"), sem("pre_trace_ready"), sem("post_trace_decayed")
        s_anew, s_atr, s_aev = sem("attention_new"), sem("attention_transposed"), sem("attention_evacuated")
        s_hmm, s_hev, s_htr, s_hst = sem("h_product"), sem("h_evacuated"), sem("h_transposed"), sem("h_in_tokens")
        s_htok = sem("h_statistics_taken")
        s_var, s_rstd, s_hb = sem("variance_ready"), sem("rstd_ready"), sem("h_plus_bias_ready")
        s_x, s_xtr, s_xT = sem("x_ready"), sem("x_transposed"), sem("xT_ready")
        s_xs, s_qk, s_v = sem("x_staged"), sem("qk_product"), sem("v_product")
        s_relu, s_bev = sem("relu_done"), sem("beta_evacuated")
        s_f, s_ftr, s_fev = sem("features_ready"), sem("features_transposed"), sem("features_evacuated")
        s_gram, s_comp = sem("gram_ready"), sem("blocks_ready")
        s_cout = [sem("blocks_stored0"), sem("blocks_stored1")]
        s_cused, s_idb = sem("blocks_read"), sem("identity_rounded")
        s_w2 = sem("second_layer_evacuated")
        s_split, s_w1 = sem("weight_split_step"), sem("weights_split")
        s_scale, s_gstep, s_gn = sem("solve_scales_ready"), sem("pool_solve_step"), sem("gn_ready")
        s_cin, s_wc, s_wout = sem("blocks_loaded"), sem("mix_weights_solved"), sem("mix_weights_stored")
        s_wt = [sem("mix_weights_loaded0"), sem("mix_weights_loaded1")]
        s_xv = [sem("x_loaded0"), sem("x_loaded1")]
        s_vp, s_vev = sem("values_projected"), sem("values_evacuated")
        s_wexp = sem("mix_weights_expanded")
        s_oT, s_oTs, s_y, s_xa = sem("out_product"), sem("out_evacuated"), sem("wo_product"), sem("residual_added")
        s_bvar, s_brstd = sem("back_variance"), sem("back_rstd")
        s_u, s_ut, s_uts = sem("mlp_in_ready"), sem("mlp_in_transposed"), sem("mlp_in_evacuated")
        s_hid, s_mlp = sem("hidden_ready"), sem("hidden_used")
        s_hot, s_res, s_out = sem("one_hot_added"), sem("result_ready"), sem("result_stored")
        s_settled = sem("wait_carried")

        block = ctx.enter_context(nc.Block())

        def settled(eng):
            eng.sem_inc(s_settled, 1)

        def store_tile(eng, t):
            eng.dma_start(out[:, t * NPT:(t + 1) * NPT, :].rearrange("t i e -> i t e"),
                          z_all[:, t * E:(t + 1) * E]).then_inc(s_out, 16)

        @block.sync
        def _(sp):
            for credit_of, n in ((s_anew, 4), (s_atr, 2), (s_aev, 2), (s_v, 2),
                                 (s_relu, 1), (s_bev, 1), (s_f, 32), (s_ftr, 16), (s_fev, 2), (s_comp, 2),
                                 (s_cout[0], 16), (s_cout[1], 16),
                                 (s_oT, 3), (s_y, 3), (s_oTs, 2), (s_wexp, 3), (s_xa, 2), (s_hid, 3),
                                 (s_vev, 1), (s_u, 1), (s_ut, 2),
                                 (s_uts, 2), (s_mlp, 2)):
                sp.sem_inc(credit_of, n)
            sp.dma_start(lat[:, 2, :], tpre.rearrange("(f p) j -> p f j", p=P)).then_inc(s_tau, 16)
            sp.dma_start(lat[:, 3, :], tpost.rearrange("(f p) j -> p f j", p=P)).then_inc(s_tau, 16)
            sp.dma_start(lat[:, 0, :], wpre.rearrange("(f p) j -> p f j", p=P)).then_inc(s_wgt, 16)
            sp.dma_start(lat[:, 1, :], wpost.rearrange("(f p) j -> p f j", p=P)).then_inc(s_wgt, 16)
            with sp.Fori(0, HALVES) as hf:
                for k in range(CH):
                    sp.wait_ge(s_anew, hf * CH + k + 1)
                    settled(sp)
                    for n, src in enumerate((pre, post, att)):
                        sp.dma_start(trace[k][n].rearrange("p (b j) -> p b j", b=SB),
                                     src[SB * k:SB * k + SB, bass.ds(hf * P, P), :].rearrange("b p j -> p b j")
                                     ).then_inc(s_trace[k], 16)
            def store_blocks(t, u):
                sp.wait_ge(s_comp, t + (1 + 2))
                settled(sp)
                sp.wait_ge(s_bev, t + (1 + 1))
                settled(sp)
                sp.dma_start(comp_d[bass.ds(t * P, P), :], comp[:, u, :]).then_inc(s_cout[u], 16)

            def by_neuron(dram, hf):
                return dram[hf * (NT * P // 2):(hf + 1) * (NT * P // 2), :].rearrange("(p s) c -> p (s c)", s=STEPS)

            def store_tiles(t0, t1):
                with sp.Fori(0, (t1 - t0) // 2) as m:
                    for u in range(2):
                        store_blocks(m * 2 + (t0 + u), u)

            def load_half(hf):
                for u in range(2):
                    sp.wait_ge(s_cout[u], hf * 64 + (64 + 16))
                if hf:
                    sp.wait_ge(s_cused, hf)
                sp.dma_start(cc[:], by_neuron(comp_d, hf)).then_inc(s_cin, 16)

            def store_mix_weights(hf):
                sp.wait_ge(s_wc, hf + 1)
                sp.dma_start(by_neuron(w_d, hf), wc[:]).then_inc(s_wout, 16)
                sp.wait_ge(s_wout, 16 * (hf + 1))

            def load_weights(p, w):
                sp.wait_ge(s_wexp, p * 2 + 1)
                settled(sp)
                for u in range(2):
                    sp.dma_start(wt[:, w, u, :], w_d[bass.ds((p * 2 + u) * P, P), :]).then_inc(s_wt[w], 16)

            def load_x(p, w):
                if p >= 2:
                    sp.wait_ge(s_vp, 2 * (p - 1))
                sp.dma_start(xv[:, w].rearrange("p u t -> p (u t)"),
                             av(xT, p * 2 * P, [1, 2 * P])).then_inc(s_xv[w], 16)

            def store(b):
                sp.wait_ge(s_res, b + 1)
                for t in range(4 * b, 4 * b + (2 if b == PAIRS // 2 - 1 else 4)):
                    store_tile(sp, t)

            store_tiles(0, NT // 2)
            load_half(0)
            store_tiles(NT // 2, NT - 2)
            store_mix_weights(0)
            for p in range(2):
                load_weights(p, p)
                load_x(p, p)
            store_blocks(NT - 2, 0)
            store_blocks(NT - 1, 1)
            load_half(1)
            for p in range(2, PAIRS):
                if p == PAIRS // 2:
                    store_mix_weights(1)
                load_weights(p, p % 2)
                load_x(p, p % 2)
                if p == PAIRS - 2:
                    store(0)
            for b in range(1, PAIRS // 2):
                store(b)
            sp.wait_ge(s_out, 16 * NT)

        @block.gpsimd
        def _(pool):
            pool.dma_start(spk_i, spk_rows.partition_broadcast(P)).then_inc(s_spk, 16)
            pool.dma_start(col_i[:], spk_cols.rearrange("(f p) b -> p f b", p=P)).then_inc(s_spk, 16)
            pool.dma_start(cst[:], consts).then_inc(s_cst, 16)
            pool.wait_ge(s_lat, 1)
            def decay(c, between=None):
                hf, k = divmod(c, CH)
                u = c % 2
                pool.wait_ge(s_trace[k], hf * 48 + 48)
                if c >= 2:
                    pool.wait_ge(s_anew, c + 3)
                nc.gpsimd.tensor_tensor(dec_post[u].rearrange("p (b j) -> p b j", b=SB),
                                        trace[k][1].rearrange("p (b j) -> p b j", b=SB),
                                        av(lat, hf * NEUR + 3 * 512, [0, SB], [1, NEUR]),
                                        ALU.mult).then_inc(s_dpost, 1)
                nc.gpsimd.tensor_tensor(new_pre[u].rearrange("p (b j) -> p b j", b=SB),
                                        trace[k][0].rearrange("p (b j) -> p b j", b=SB),
                                        av(lat, hf * NEUR + 2 * 512, [0, SB], [1, NEUR]), ALU.mult)
                nc.gpsimd.tensor_tensor(inc_pre[u].rearrange("p (b j) -> p b j", b=SB),
                                        av(spk_f, SB * k * NEUR, [NEUR, SB], [1, NEUR]),
                                        av(lat, hf * NEUR, [0, SB], [1, NEUR]), ALU.mult).then_inc(s_prod, 1)
                if between:
                    between()
                if c not in DVE_ADDS:
                    pool.wait_ge(s_prod, c + 1)
                    nc.gpsimd.tensor_tensor(new_pre[u], new_pre[u], inc_pre[u], ALU.add).then_inc(s_pre, 1)

            def h_rstd(g):
                pool.wait_ge(s_var, g + 1)
                nc.gpsimd.tensor_tensor(rstd[:, g % 2, :], veps[:, g % 2, :], mhalf[:], ALU.pow).then_inc(s_rstd, 1)

            def h_bias(g):
                pool.wait_ge(s_hst, g + 1)
                nc.gpsimd.tensor_tensor(av(hb_tok, g * 512, [E, 4], [1, E]),
                                        h_st[:, g % 2, :].rearrange("p (t e) -> p t e", e=E),
                                        av(bet, 0, [0, 4], [1, E]), ALU.add).then_inc(s_hb, 1)

            for c in range(2 * CH - 2):
                decay(c)
            decay(2 * CH - 2, lambda: h_rstd(0))
            decay(2 * CH - 1)
            pool.wait_ge(s_w, 16 * 7)
            h_bias(0)
            for g in range(1, GROUPS):
                h_rstd(g)
                h_bias(g)

            for n in range(SPLIT - 1):
                nc.gpsimd.tensor_copy(w1b[:], w1s[:]).then_inc(s_split, 1)
                pool.wait_ge(s_split, 3 * n + 1)
                nc.gpsimd.tensor_tensor(w1b[:], w1b[:], av(cst, C_PART + n, [0, 3 * HC], parts=GIN),
                                        ALU.mult).then_inc(s_split, 1)
                pool.wait_ge(s_split, 3 * n + 2)
                nc.gpsimd.tensor_tensor(w1s[:], w1s[:], w1b[:], ALU.subtract).then_inc(s_split, 1)
                pool.wait_ge(s_split, 3 * n + 3)
            nc.gpsimd.tensor_copy(w1b[:], w1s[:]).then_inc(s_w1, 1)

            def form_gn(hf):
                pool.wait_ge(s_scale, hf + 1)
                gv = gn[:].rearrange("p (t h s) -> p t h s", t=STEPS, h=HEADS)
                nc.gpsimd.tensor_tensor(gv, av(cc, 0, [1, STEPS], [16, HEADS], [COMP, STEPS]),
                                        av(rsum, 0, [0, STEPS], [2, HEADS], [2 * HEADS, STEPS]),
                                        ALU.mult).then_inc(s_gstep, 1)
                pool.wait_ge(s_gstep, hf + 1)
                nc.gpsimd.tensor_tensor(gv, gv, av(bk, 0, [HEADS, STEPS], [1, HEADS], [0, STEPS]),
                                        ALU.mult).then_inc(s_gn, 1)

            def expand(p, w, u):
                if u == 0:
                    pool.wait_ge(s_wt[w], (p - w) * 16 + 32)
                    pool.wait_ge(s_oT, p * 2 + 1)
                nc.gpsimd.tensor_tensor(wexp[:, w, u].rearrange("p h (i t) -> p h i t", t=STEPS),
                                        av(wt, (2 * w + u) * 64, [STEPS, HEADS], [0, NPT], [1, STEPS]),
                                        av(cst, C_M16, [0, HEADS], [1, NPT], [0, STEPS]),
                                        ALU.mult).then_inc(s_wexp, 1)

            def power(p, n):
                pool.wait_ge(s_bvar, p * 2 + (n + 1))
                nc.gpsimd.tensor_tensor(rstd[:, n, 0:2], veps[:, n, 0:2], mhalf[:, 0:2], ALU.pow).then_inc(s_brstd, 1)

            def serve(p, w, between=None):
                power(p, 0)
                power(p, 1)
                if between is not None:
                    form_gn(between)
                expand(p + 2, w, 0)
                expand(p + 2, w, 1)

            def add_h2(b):
                pool.wait_ge(s_hot, b + 1)
                settled(pool)
                zb = av(z_all, b * 4 * E, [1, 4 * E])
                nc.gpsimd.tensor_tensor(zb, zb, av(h2_all, b * 4 * E, [1, 4 * E]), ALU.add).then_inc(s_res, 1)

            form_gn(0)
            pool.wait_ge(s_hmm, GROUPS)
            for p in range(2):
                expand(p, p, 0)
                expand(p, p, 1)
            serve(0, 0, between=1)
            serve(1, 1)
            with pool.Fori(0, PAIRS // 2 - 2) as m:
                for w in range(2):
                    serve(m * 2 + (w + 2), w)
                add_h2(m)
            for p in range(PAIRS - 2, PAIRS):
                power(p, 0)
                power(p, 1)
            add_h2(PAIRS // 2 - 2)

        @block.scalar
        def _(act):
            act.wait_ge(s_tau, 32)
            nc.scalar.activation(lat[:, 2:4, :], lat[:, 2:4, :], ACT.Exp, scale=-1.0).then_inc(s_exp, 1)
            act.wait_ge(s_exp, 1)
            nc.scalar.activation(lat[:, 2:4, :], lat[:, 2:4, :], ACT.Exp, scale=-DT).then_inc(s_exp, 1)
            act.wait_ge(s_wgt, 32)
            nc.scalar.activation(lat[:, 0:2, :], lat[:, 0:2, :], ACT.Exp).then_inc(s_exp, 1)
            act.dma_start(vw[:], vwT.rearrange("(c p) e -> p c e", p=P)).then_inc(s_w, 16)
            act.dma_start(vbias[:], vb).then_inc(s_w, 16)
            act.dma_start(wqkv[:], wqkvT).then_inc(s_w, 16)
            act.dma_start(wo[:], woT.rearrange("(c p) e -> p c e", p=P)).then_inc(s_w, 16)
            act.dma_start(gam[:], lng.partition_broadcast(P)).then_inc(s_w, 16)
            act.dma_start(bet[:], lnb.partition_broadcast(P)).then_inc(s_w, 16)
            act.dma_start(w1s[:], w1).then_inc(s_w, 16)

            def evacuate_attention(c):
                hf, k = divmod(c, CH)
                act.wait_ge(s_atr, c + (1 + 2))
                for b in range(SB):
                    last = nc.scalar.activation(
                        av(attT, hf * (P * STEPS) + SB * k + b, [NEUR * STEPS, 2], [STEPS, P]),
                        ptr[:, c % 2, b * NEUR:(b + 1) * NEUR].rearrange("p (c i) -> p c i", c=2), ACT.Copy)
                last.then_inc(s_aev, 1)

            def evacuate_h(g):
                act.wait_ge(s_hmm, g + 1)
                if g >= 2:
                    act.wait_ge(s_htr, g - 1)
                nc.scalar.activation(hT[:, g % 2, :], pgr[:, g % 2, :], ACT.Identity,
                                     bias=vbias[:]).then_inc(s_hev, 1)

            def keep_h(g):
                act.wait_ge(s_htr, g + 1)
                if g >= 2:
                    act.wait_ge(s_hb, g - 1)
                    act.wait_ge(s_x, g - 1)
                nc.scalar.activation(h_st[:, g % 2, :], pms[:], ACT.Copy).then_inc(s_hst, 1)

            def keep_x(g):
                act.wait_ge(s_x, g + 1)
                nc.scalar.activation(av(x_tok, g * 512, [1, 512]), x_st[:, g % 2, :], ACT.Copy)
                act.wait_ge(s_xtr, g + 1)
                nc.scalar.activation(av(xT, g * 512, [1, 512]), pms[:], ACT.Copy).then_inc(s_xT, 1)
                act.wait_ge(s_xT, g + 1)

            def stage(t, u):
                act.wait_ge(s_v, t + 1)
                nc.scalar.activation(xs[:, u, :], av(xT, t * P, [1, P]), ACT.Copy).then_inc(s_xs, 1)

            def evacuate_qkv(t, u):
                xv = X[:, u, :].rearrange("p (j w) -> p j w", w=XW)
                qk = pqk[:].rearrange("p (j d) -> p j d", d=DH)
                act.wait_ge(s_f, t * 16 + 16)
                for n, js in enumerate((slice(0, HEADS), slice(HEADS, 2 * HEADS))):
                    act.wait_ge(s_qk, t * 2 + (n + 1))
                    for first, sign in ((2, 1.0), (2 + DH, -1.0)):
                        nc.scalar.activation(xv[:, js, first:first + DH], qk[:, js], ACT.Relu, scale=sign)
                        yield
                nc.scalar.activation(xv[:, :, 0:2], qk[:, :, DH - 2:DH], ACT.Relu, scale=-1.0).then_inc(s_relu, 1)
                yield
                act.wait_ge(s_v, t + (1 + 2))
                act.wait_ge(s_cout[u], (t - u) * 8 + 16)
                nc.scalar.activation(comp[:, u, OFF_BETA:COMP], pms[:, 0:HEADS], ACT.Exp,
                                     scale=-1.0).then_inc(s_bev, 1)
                yield

            def evacuate_tile(t, u, last=False):
                qkv = evacuate_qkv(t + 1, 1 - u)
                evacuate_features(t, heads=range(1))
                some(qkv, 3)
                evacuate_features(t, qkv, range(1, 3))
                evacuate_features(t, heads=range(3, 5))
                if not last:
                    stage(t + 2, u)
                evacuate_features(t, heads=range(5, 7))
                some(qkv, 1)
                evacuate_features(t, heads=range(7, HEADS))

            def evacuate_features(t, between=iter(()), heads=range(HEADS)):
                for h in heads:
                    act.wait_ge(s_ftr, t * 8 + (16 + h + 1))
                    nc.scalar.activation(FT[:, h].rearrange("p r q t -> p (r q t)"), ptr[:, h % 2, :],
                                         ACT.Copy).then_inc(s_fev, 1)
                    next(between, None)

            def some(steps, n):
                for _ in range(n):
                    next(steps)

            for c in range(CH):
                evacuate_attention(c)
            act.wait_ge(s_w, 16 * 7)
            evacuate_h(0)
            keep_h(0)
            evacuate_attention(CH)
            evacuate_h(1)
            evacuate_attention(CH + 1)
            keep_x(0)
            stage(0, 0)
            stage(1, 1)
            keep_h(1)
            qkv = evacuate_qkv(0, 0)
            some(qkv, 3)
            evacuate_attention(CH + 2)
            some(qkv, 3)
            qkv_1 = evacuate_qkv(1, 1)
            some(qkv_1, 2)
            evacuate_attention(CH + 3)
            some(qkv_1, 2)
            keep_x(1)
            some(qkv_1, 1)
            evacuate_h(2)
            evacuate_features(0, heads=range(1))
            keep_h(2)
            evacuate_features(0, heads=range(1, 2))
            stage(2, 0)
            evacuate_features(0, heads=range(2, 4))
            evacuate_h(3)
            evacuate_features(0, heads=range(4, 6))
            some(qkv_1, 1)
            evacuate_features(0, heads=range(6, HEADS))
            keep_x(2)
            qkv = evacuate_qkv(2, 0)
            evacuate_features(1, qkv, range(2))
            keep_h(3)
            evacuate_features(1, qkv, range(2, 5))
            evacuate_features(1, heads=range(5, 6))
            some(qkv, 1)
            stage(3, 1)
            evacuate_features(1, heads=range(6, 7))
            keep_x(3)
            evacuate_features(1, heads=range(7, HEADS))
            with act.Fori(0, NT // 2 - 2) as m:
                t0 = m * 2
                for u in range(2):
                    evacuate_tile(t0 + (u + 2), u)
            evacuate_tile(NT - 2, 0, last=True)
            evacuate_features(NT - 1)

            def evacuate_out(p, w):
                for u in range(2):
                    act.wait_ge(s_oT, p * 2 + (u + 1 + 3))
                    act.wait_ge(s_y, p * 2 + 1)
                    nc.scalar.activation(oT[:, w, u].rearrange("p c t -> p (c t)"), ptr[:, u, :],
                                         ACT.Copy).then_inc(s_oTs, 1)

            def evacuate_values(p, w):
                act.wait_ge(s_oT, p * 2 + 1)
                for u in range(2):
                    act.wait_ge(s_vp, p * 2 + (u + 1))
                    nc.scalar.activation(vs[:, w, u, :], pgr[:, u, :], ACT.Copy).then_inc(s_vev, 1)

            def evacuate_mlp_in(p, w):
                act.wait_ge(s_ut, p + (1 + 2))
                act.wait_ge(s_hid, p * 2 + 1)
                nc.scalar.activation(UT[:, w].rearrange("k u t -> k (u t)"), pback[w][0:GIN, 2 * P:4 * P],
                                     ACT.Copy).then_inc(s_uts, 1)
                for u in range(2):
                    act.wait_ge(s_hid, p * 2 + (u + 1 + 3))
                    nc.scalar.activation(w2c[:, u, :], phid[u][:, 2 * HC:3 * HC], ACT.Copy).then_inc(s_w2, 1)

            evacuate_values(0, 0)
            evacuate_out(0, 0)
            evacuate_values(1, 1)
            with act.Fori(0, PAIRS // 2 - 1) as m:
                for w in range(2):
                    evacuate_out(m * 2 + (w + 1), 1 - w)
                    evacuate_values(m * 2 + (w + 2), w)
                    evacuate_mlp_in(m * 2 + w, w)
            evacuate_out(PAIRS - 1, 1)
            evacuate_mlp_in(PAIRS - 2, 0)
            evacuate_mlp_in(PAIRS - 1, 1)
            act.wait_ge(s_res, PAIRS // 2)
            for t in range(NT - 2, NT):
                store_tile(act, t)

        @block.vector
        def _(dve):
            count = [0, 0]

            def step(ins):
                ins.then_inc(s_dve, 1)
                count[1] += 1
                return count[0] + count[1]

            def link(ins, meanwhile=iter(())):
                done = step(ins)
                next(meanwhile, None)
                dve.wait_ge(s_dve, done)

            nc.vector.memset(mhalf[:], -0.5)
            nc.vector.memset(Ub[:], 1.0)
            nc.vector.memset(nn[:], 0.0)
            link(nc.vector.memset(inv[:], 0.0))
            nc.vector.memset(av(inv, 0, [65, STEPS], [8, HEADS]), 1.0)
            dve.wait_ge(s_cst, 16)
            nc.vector.tensor_copy(ident_b[:], ident).then_inc(s_idb, 1)
            dve.wait_ge(s_spk, 32)
            nc.vector.tensor_copy(spk_f, spk_i)
            nc.vector.tensor_scalar(spk_m, spk_i, 0.0, None, ALU.not_equal)
            nc.vector.tensor_copy(col_f[:], col_i[:])
            nc.vector.tensor_scalar(col_m[:], col_i[:], 0.0, None, ALU.not_equal)
            dve.wait_ge(s_exp, 3)
            link(nc.vector.tensor_scalar(lat[:, 0:2, :], lat[:, 0:2, :], DT, None, ALU.mult))
            nc.vector.memset(rstd[:], 0.0).then_inc(s_lat, 1)

            def form_attention(c, between=None):
                hf, k = divmod(c, CH)
                u = c % 2

                def halves(out_, in0, col, in1, in0_fixed=None, op=ALU.add):
                    for b in range(SB):
                        js = slice(b * NEUR, (b + 1) * NEUR)
                        last = nc.vector.scalar_tensor_tensor(
                            out_[:, js], in0_fixed if in0_fixed is not None else in0[:, js],
                            av(col, hf * STEPS + SB * k + b, [1, 1]), in1[:, js], ALU.mult, op)
                    return last

                dve.wait_ge(s_dpost, c + 1)
                link(halves(new_post, None, col_f, dec_post[u], av(lat, hf * NEUR + 512, [1, NEUR])))
                link(nc.vector.tensor_tensor(mix, new_post, spk_m[:, SB * k * NEUR:SB * (k + 1) * NEUR], ALU.mult))
                if c in DVE_ADDS:
                    dve.wait_ge(s_prod, c + 1)
                    link(nc.vector.tensor_tensor(new_pre[u], new_pre[u], inc_pre[u], ALU.add))
                else:
                    dve.wait_ge(s_pre, c + 1 - sum(n < c for n in DVE_ADDS))
                link(halves(mix, new_pre[u], col_m, mix))
                dve.wait_ge(s_trace[k], hf * 48 + 48)
                link(nc.vector.scalar_tensor_tensor(new_post, mix, 1.0, trace[k][2], ALU.subtract, ALU.mult))
                if between:
                    between()
                dve.wait_ge(s_atr, c + 1)
                link(halves(anew[u], new_pre[u], col_m, new_post, op=ALU.subtract))
                nc.vector.tensor_scalar(anew[u], anew[u], -0.5, 1.5, ALU.max, ALU.min).then_inc(s_anew, 1)

            def h_statistics(g):
                u = g % 2
                dve.wait_ge(s_hst, g + 1)
                for t in range(4):
                    last = nc.vector.bn_stats(stat[:, t, :], h_st[:, u, t * E:(t + 1) * E])
                last.then_inc(s_htok, 1)
                dve.wait_ge(s_htok, g + 1)
                for t in range(4):
                    last = nc.vector.bn_aggr(mv[:, u, t, :], stat[:, t, :])
                link(last)
                nc.vector.tensor_scalar(veps[:, u, :], mv[:, u, :, 1], EPS, None, ALU.add).then_inc(s_var, 1)

            def h_normalise(g):
                u = g % 2
                dve.wait_ge(s_rstd, g + 1)
                if g >= 2:
                    dve.wait_ge(s_xT, g - 1)
                for t in range(4):
                    last = nc.vector.tensor_scalar(x_st[:, u, t * E:(t + 1) * E], h_st[:, u, t * E:(t + 1) * E],
                                                   mv[:, u, t, 0:1], rstd[:, u, t:t + 1], ALU.subtract, ALU.mult)
                last.then_inc(s_x, 1)

            for c in range(CH + 1):
                form_attention(c)
            form_attention(CH + 1, lambda: h_statistics(0))
            h_normalise(0)
            form_attention(CH + 2)
            h_statistics(1)
            form_attention(CH + 3)
            h_normalise(1)

            def features(t, u, js=range(2 * HEADS), between=None):
                dve.wait_ge(s_relu, t + (1 + 1))
                dve.wait_ge(s_ftr, t * 8 + 8)
                dve.wait_ge(s_cout[u], (t - u) * 8 + 16)
                for j in js:
                    if between and j == BLOCKS_AT:
                        between()
                    base = u * 2 * HEADS * XW + j * XW
                    nc.vector.scalar_tensor_tensor(
                        F[:, u, j * FEAT:(j + 1) * FEAT].rearrange("p (r d) -> p r d", r=2),
                        av(X, base + 2, [0, 2], [1, 2 * DH]), 1.0, av(X, base, [1, 2], [1, 2 * DH]),
                        ALU.mult, ALU.mult,
                        accum_out=comp[:, u, OFF_SUM + j:OFF_SUM + j + 1]).then_inc(s_f, 1)

            def blocks(t, u):
                dve.wait_ge(s_comp, t + 2)
                dve.wait_ge(s_gram, t + 1)
                link(nc.vector.tensor_tensor(gmask[:].rearrange("p (j i t) -> p j i t", i=QW, t=STEPS),
                                             pgr[:, u, :].rearrange("p (j i t) -> p j i t", i=QW, t=STEPS),
                                             av(cst, C_M4, [0, 2 * HEADS], [1, QW], [0, STEPS]), ALU.mult))
                nc.vector.tensor_reduce(comp[:, u, 0:OFF_SUM].rearrange("p (j t) -> p j t", t=STEPS),
                                        av(gmask, 0, [32, 2 * HEADS], [1, STEPS], [STEPS, QW]), AX_X,
                                        ALU.add).then_inc(s_comp, 1)

            T3 = STEPS * HEADS

            def solve_setup(hf):
                if hf:
                    dve.wait_ge(s_wc, hf)
                dve.wait_ge(s_cin, hf * 16 + 16)
                ccv = cc[:].rearrange("p (s c) -> p s c", c=COMP)
                nc.vector.reciprocal(rsum[:], ccv[:, :, OFF_SUM:OFF_BETA])
                link(nc.vector.tensor_scalar(beta[:], ccv[:, :, OFF_BETA:COMP], 1.0, None, ALU.add))
                rk = av(rsum, 0, [0, STEPS], [2, HEADS], [2 * HEADS, STEPS])
                an_v = an[:].rearrange("p (t h s) -> p t h s", t=STEPS, h=HEADS)
                link(nc.vector.reciprocal(beta[:], beta[:]))
                nc.vector.tensor_tensor(bk[:], beta[:], av(rsum, 0, [2 * HEADS, STEPS], [2, HEADS]),
                                        ALU.mult).then_inc(s_scale, 1)
                link(nc.vector.tensor_tensor(an_v, av(cc, 8, [1, STEPS], [16, HEADS], [COMP, STEPS]), rk, ALU.mult))
                link(nc.vector.tensor_tensor(an_v, an_v, av(rsum, 1, [2 * HEADS, STEPS], [2, HEADS], [0, STEPS]),
                                             ALU.mult))
                link(nc.vector.tensor_tensor(an_v, an_v, av(cst, C_CAUS, [STEPS, STEPS], [0, HEADS], [1, STEPS]),
                                             ALU.mult))
                link(nc.vector.tensor_reduce(den[:], an[:].rearrange("p (a s) -> p a s", s=STEPS), AX_X, ALU.add))
                link(nc.vector.tensor_scalar(den[:], den[:], EPS, None, ALU.add))
                link(nc.vector.reciprocal(den[:], den[:]))
                link(nc.vector.tensor_scalar(den[:], den[:], float(DH) ** -0.5, None, ALU.mult))
                dve.wait_ge(s_gn, hf + 1)
                dve.sem_inc(s_cused, 1)

            def products(b, coef, t, n):
                return nc.vector.tensor_tensor(av(prod, b * 512, [n * n, HEADS], [n, n], [1, n]),
                                               av(inv, 0, [8, HEADS], [1, n], [T3, n]),
                                               av(coef, t * T3, [8, HEADS], [0, n], [1, n]), ALU.mult)

            def row(dst, b, t, n, negate):
                return nc.vector.tensor_reduce(av(dst, t * T3, [8, HEADS], [1, n]),
                                               av(prod, b * 512, [n * n, HEADS], [n, n], [1, n]), AX_X, ALU.add,
                                               negate=negate)

            def solve_rows(t):
                products(0, gn, t, t)
                link(products(1, an, t - 1, t))
                row(inv, 0, t, t, True)
                link(row(nn, 1, t - 1, t, False))

            def solve_end(hf):
                if hf:
                    dve.wait_ge(s_wout, 16 * hf)
                link(products(1, an, STEPS - 1, STEPS))
                link(row(nn, 1, STEPS - 1, STEPS, False))
                link(nc.vector.tensor_tensor(nn[:].rearrange("p (a u) -> p a u", u=STEPS),
                                             nn[:].rearrange("p (a u) -> p a u", u=STEPS),
                                             av(den, 0, [1, STEPS * HEADS], [0, STEPS]), ALU.mult))
                nc.vector.tensor_tensor(wc[:].rearrange("p (u h t) -> p u h t", u=STEPS, h=HEADS),
                                        av(nn, 0, [1, STEPS], [8, HEADS], [T3, STEPS]),
                                        av(beta, 0, [HEADS, STEPS], [1, HEADS], [0, STEPS]),
                                        ALU.mult).then_inc(s_wc, 1)

            def looped(passes, links):
                assert count[1] - before == links, count[1] - before
                count[:] = [0, before + passes * links]

            HT = NT // 2
            BLOCKS_AT = 14
            dve.wait_ge(s_atr, 2 + CH * HALVES)
            features(0, 0)
            h_statistics(2)
            features(1, 1, range(HEADS))
            h_normalise(2)
            features(1, 1, range(HEADS, 2 * HEADS))
            blocks(0, 0)
            h_statistics(3)
            h_normalise(3)
            features(2, 0, between=lambda: blocks(1, 1))
            before = count[1]
            with dve.Fori(0, HT // 2 - 1) as m:
                t0 = m * 2
                count[0] = t0
                for u in range(2):
                    features(t0 + (u + 3), 1 - u, between=lambda: blocks(t0 + (u + 2), u))
            looped(HT // 2 - 1, 2)
            features(HT + 1, 1, between=lambda: blocks(HT, 0))
            solve_setup(0)
            rows = iter(range(1, STEPS))
            for t, rows_now in enumerate((3, 2, 1, 1, 0, 0), 1):
                features(HT + 1 + t, 1 - t % 2, between=lambda: blocks(HT + t, t % 2))
                for _ in range(rows_now):
                    solve_rows(next(rows))
                if t == STEPS - 3:
                    solve_end(0)
            blocks(NT - 1, 1)

            def w2v(t):
                return t.rearrange("p (u e) -> p u e", u=2)

            def stats(src, n, meanwhile):
                for u in range(2):
                    last = nc.vector.bn_stats(stat[:, u, :], src[:, u * E:(u + 1) * E])
                link(last, meanwhile if n else iter(()))
                settled(dve)
                for u in range(2):
                    last = nc.vector.bn_aggr(mv[:, n, u, :], stat[:, u, :])
                link(last, meanwhile if n else iter(()))
                nc.vector.tensor_scalar(veps[:, n, 0:2], mv[:, n, 0:2, 1], EPS, None, ALU.add).then_inc(s_bvar, 1)

            def second_layer(p, w):
                dve.wait_ge(s_mlp, p * 2 + 2)
                for u in range(2):
                    dve.wait_ge(s_w2, p * 2 + (u + 1))
                    for r in range(2):
                        n = u * 2 + r
                        last = nc.vector.scalar_tensor_tensor(
                            junk[:, n, :], phid[u][:, r * HC:(r + 1) * HC], 0.0, w2c[:, u, :], ALU.max, ALU.mult,
                            accum_out=y[:, w * 4 + n:w * 4 + n + 1])
                        if r:
                            last.then_inc(s_mlp, 1)
                        yield

            def mlp_results(b):
                zb = b * 4 * E
                flags = step(nc.vector.tensor_scalar(opm[:], av(z_all, zb + 1, [E, 4], [1, 3]), 0.5, None, ALU.is_gt))
                yield
                nc.vector.tensor_scalar(act2[:], av(z_all, zb, [E, 4]), 0.5, 2.0, ALU.is_ge, ALU.mult)
                dve.wait_ge(s_mlp, b * 4 + (4 + 2))
                clipped = step(nc.vector.tensor_scalar(res[:], y[:], -1.0, 16.0, ALU.max, ALU.min))
                yield
                dve.wait_ge(s_dve, flags)
                found = step(nc.vector.tensor_reduce(anyop[:], opm[:], AX_X, ALU.max))
                yield
                dve.wait_ge(s_dve, clipped)
                rounded = step(nc.vector.tensor_scalar(res[:], res[:], ROUND, ROUND, ALU.add, ALU.subtract))
                yield
                dve.wait_ge(s_dve, found)
                step(nc.vector.tensor_tensor(act2[:], act2[:], anyop[:], ALU.mult))
                yield
                dve.wait_ge(s_dve, rounded)
                done[0] = step(nc.vector.tensor_scalar(res[:], res[:], 0.0, 15.0, ALU.max, ALU.min))
                yield

            def finish(b, last=False):
                zb = b * 4 * E
                zo = av(z_all, zb + 80, [E, 4], [1, 32])
                hv = hot[:].rearrange("p (v k) -> p v k", k=32)
                hit = step(nc.vector.tensor_tensor(hot[:].rearrange("p (a k) -> p a k", k=16),
                                                   av(cst, C_IOTA, [0, 8], [1, 16]), av(res, 0, [1, 8], [0, 16]),
                                                   ALU.is_equal))
                yield
                dve.wait_ge(s_dve, hit)
                hit = step(nc.vector.tensor_tensor(hv, hv, av(act2, 0, [1, 4], [0, 32]), ALU.mult))
                yield
                dve.wait_ge(s_dve, hit)
                nc.vector.tensor_tensor(zo, zo, hv, ALU.add).then_inc(s_hot, 1)
                yield
                if not last:
                    return
                dve.wait_ge(s_hot, PAIRS // 2)
                dve.wait_ge(s_res, PAIRS // 2 - 1)
                nc.vector.tensor_tensor(av(z_all, zb, [1, 4 * E]), av(h2_all, zb, [1, 4 * E]),
                                        av(z_all, zb, [1, 4 * E]), ALU.add).then_inc(s_res, 1)
                yield

            def some(steps, n):
                for _ in range(n):
                    next(steps, None)

            def put(col, n, src):
                stride = 5 if col < FLAG0 else 3
                return nc.vector.tensor_copy(av(Ub, col, [ROWS, 2], [stride, SPLIT], [1, n]), src)

            def two_norms(p, w, others):
                z0 = p * 2 * E
                dve.wait_ge(s_y, p * 2 + (2 + 3))
                nc.vector.tensor_tensor(xa[:], av(x_tok, z0, [1, 2 * E]), pback[w][:, 0:2 * E],
                                        ALU.add).then_inc(s_xa, 1)
                dve.wait_ge(s_xa, p + (1 + 2))
                stats(xa, 0, others)
                for u in range(2):
                    last = nc.vector.scalar_tensor_tensor(xn[:, u * E:(u + 1) * E], xa[:, u * E:(u + 1) * E],
                                                          mv[:, 0, u, 0:1], gam[:], ALU.subtract, ALU.mult)
                scaled = step(last)
                some(others, 2)
                dve.wait_ge(s_dve, scaled)
                dve.wait_ge(s_brstd, p * 2 + 1)
                for u in range(2):
                    last = nc.vector.scalar_tensor_tensor(av(h2_all, z0 + u * E, [1, E]),
                                                          xn[:, u * E:(u + 1) * E], rstd[:, 0, u:u + 1],
                                                          av(hb_tok, z0 + u * E, [1, E]), ALU.mult, ALU.add)
                link(last, others)
                settled(dve)
                stats(av(h2_all, z0, [1, 2 * E]), 1, others)
                some(others, 3)
                dve.wait_ge(s_brstd, p * 2 + 2)
                for u in range(2):
                    last = nc.vector.tensor_scalar(av(z_all, z0 + u * E, [1, E]), av(h2_all, z0 + u * E, [1, E]),
                                                   mv[:, 1, u, 0:1], rstd[:, 1, u:u + 1], ALU.subtract, ALU.mult)
                link(last, others)
                flags = av(z_all, z0 + 1, [E, 2], [1, 3])
                bit = step(nc.vector.scalar_tensor_tensor(w2v(bits[:]), av(z_all, z0 + 16, [E, 2], [1, 64]), 0.5,
                                                          av(cst, C_RAMP, [0, 2], [1, 64]), ALU.is_gt, ALU.mult))
                dve.wait_ge(s_u, p + 1)
                step(nc.vector.tensor_scalar(om[:], flags, 0.5, None, ALU.is_gt))
                others_off = step(nc.vector.tensor_scalar(no[:], flags, 0.5, None, ALU.is_le))
                dve.wait_ge(s_dve, bit)
                first = step(nc.vector.tensor_reduce(top[:], bits[:].rearrange("p (n b) -> p n b", b=16), AX_X,
                                                     ALU.max))
                part = step(put(FLAG0, 3, av(z_all, z0 + 1, [E, 2], [0, SPLIT], [1, 3])))
                dve.wait_ge(s_dve, others_off)
                step(nc.vector.tensor_tensor(om[:, :, 1], om[:, :, 1], no[:, :, 0], ALU.mult))
                dve.wait_ge(s_dve, first)
                rest = step(nc.vector.tensor_scalar(rem[:], top[:], -1.0, 16.0, ALU.mult, ALU.add))
                step(nc.vector.tensor_tensor(om[:, :, 2], no[:, :, 0], no[:, :, 1], ALU.mult))
                dve.wait_ge(s_dve, part)
                left = step(nc.vector.tensor_tensor(flag[:], flags, Ub[:, :, FLAG0:FLAG0 + 3], ALU.subtract))
                dve.wait_ge(s_dve, rest)
                found = step(nc.vector.scalar_tensor_tensor(nib[:], top[:].rearrange("p (u n) -> p u n", u=2), 0.0,
                                                            rem[:].rearrange("p (u n) -> p u n", u=2), ALU.is_gt,
                                                            ALU.mult))
                dve.wait_ge(s_dve, left)
                part = step(put(FLAG0 + 3 * SPLIT, 3, av(flag, 0, [3, 2], [0, SPLIT], [1, 3])))
                dve.wait_ge(s_dve, found)
                step(put(0, 4, av(nib, 0, [4, 2], [0, SPLIT], [1, 4])))
                dve.wait_ge(s_dve, part)
                link(nc.vector.tensor_tensor(flag[:], flag[:],
                                             Ub[:, :, FLAG0 + 3 * SPLIT:FLAG0 + 3 * SPLIT + 3], ALU.subtract), others)
                link(put(FLAG0 + 6 * SPLIT, 3, av(flag, 0, [3, 2], [0, SPLIT], [1, 3])), others)
                dve.wait_ge(s_ut, p + 1)
                nc.vector.tensor_tensor(U[:, w], av(Ub, 0, [ROWS, 2], [0, OPS], [1, ROWS]),
                                        av(om, 0, [OPS, 2], [1, OPS], [0, ROWS]), ALU.mult).then_inc(s_u, 1)
                for _ in others:
                    pass

            done = [0]

            def back(p, w, batch=iter(())):
                def others():
                    yield from second_layer(p - 1, 1 - w)
                    yield from batch
                two_norms(p, w, others())

            two_norms(0, 0, iter(()))
            solve_setup(1)
            for t in range(1, STEPS):
                solve_rows(t)
            solve_end(1)
            back(1, 1)
            back(2, 0, mlp_results(0))
            before = count[1]
            with dve.Fori(0, PAIRS // 2 - 2) as m:
                count[0] = m * TWO_PAIRS
                back(m * 2 + 3, 1, finish(m))
                back(m * 2 + 4, 0, mlp_results(m + 1))
            looped(PAIRS // 2 - 2, TWO_PAIRS)
            back(PAIRS - 1, 1, finish(PAIRS // 2 - 2))
            for steps in (second_layer(PAIRS - 1, 1), mlp_results(PAIRS // 2 - 1)):
                for _ in steps:
                    pass
            dve.wait_ge(s_dve, done[0])
            for _ in finish(PAIRS // 2 - 1, last=True):
                pass

        @block.tensor
        def _(pe):
            mm, tr = nc.tensor.matmul, nc.tensor.transpose
            pe.wait_ge(s_cst, 16)

            def transpose_attention(c):
                pe.wait_ge(s_anew, c + (1 + 4))
                pe.wait_ge(s_aev, c + 1)
                for n in range(4):
                    last = tr(ptr[:, c % 2, n * P:(n + 1) * P], anew[c % 2][:, n * P:(n + 1) * P], ident)
                last.then_inc(s_atr, 1)

            def h_product(g):
                pe.wait_ge(s_aev, 2 + CH * (1 + g // 2))
                if g >= 2:
                    pe.wait_ge(s_hev, g - 1)
                for c in range(2):
                    last = mm(pgr[:, g % 2, :], vw[:, c, :], av(attT, g * 512 + c * NEUR * STEPS, [1, 512]),
                              start=(c == 0), stop=(c == 1))
                last.then_inc(s_hmm, 1)

            def h_transpose(g, betas=0):
                pe.wait_ge(s_hev, g + 1)
                if g:
                    pe.wait_ge(s_xT, g)
                if betas:
                    pe.wait_ge(s_bev, betas + 1)
                for t in range(4):
                    last = tr(pms[:, t * P:(t + 1) * P], hT[:, g % 2, t * P:(t + 1) * P], ident)
                last.then_inc(s_htr, 1)

            def x_transpose(g, betas=0):
                pe.wait_ge(s_x, g + 1)
                if betas:
                    pe.wait_ge(s_bev, betas + 1)
                for t in range(4):
                    last = tr(pms[:, t * P:(t + 1) * P], x_st[:, g % 2, t * P:(t + 1) * P], ident)
                last.then_inc(s_xtr, 1)

            def project_qk(t, u):
                pe.wait_ge(s_xs, t + 1)
                pe.wait_ge(s_relu, t + 1)
                for n in range(2):
                    mm(pqk[:, n * 512:(n + 1) * 512], xs[:, u, :], wqkv[:, n * 512:(n + 1) * 512],
                       start=True, stop=True).then_inc(s_qk, 1)

            def project_beta(t, u):
                pe.wait_ge(s_bev, t + 1)
                mm(pms[:, 0:HEADS], xs[:, u, :], wqkv[:, 1536:1544], start=True, stop=True).then_inc(s_v, 1)

            def gram(t, u, h):
                pe.wait_ge(s_fev, t * 8 + (h + 1 + 2))
                if h == 0:
                    pe.wait_ge(s_comp, t + 1)
                for g in range(NQ):
                    for r in range(2):
                        last = mm(pgr[32 * g:32 * g + 32, u, h * 64:(h + 1) * 64], FT[:, h, r, 0, 32 * g:32 * g + 32],
                                  av(FT, h * 512 + r * 256 + 32 * g, [P, 2], [1, 32]), start=(r == 0), stop=(r == 1))
                if h == HEADS - 1:
                    last.then_inc(s_gram, 1)

            def transpose_head(t, u, h):
                pe.wait_ge(s_f, t * 16 + (32 + 2 * h + 2))
                pe.wait_ge(s_fev, t * 8 + (h + 1))
                for r in range(2):
                    for q in range(2):
                        src = (2 * h + q) * FEAT + r * 2 * DH
                        last = tr(ptr[:, h % 2, (2 * r + q) * P:(2 * r + q + 1) * P], F[:, u, src:src + P], ident)
                last.then_inc(s_ftr, 1)

            def head(t, u, h):
                transpose_head(t, u, h)
                gram(t, u, h - 1)

            def front(t, u):
                transpose_head(t, u, 0)
                project_qk(t + 1, 1 - u)
                project_beta(t + 1, 1 - u)
                gram(t - 1, 1 - u, HEADS - 1)
                for h in range(1, HEADS):
                    head(t, u, h)

            for c in range(CH):
                transpose_attention(c)
            pe.wait_ge(s_w, 16 * 7)
            h_product(0)
            h_transpose(0)
            transpose_attention(CH)
            h_product(1)
            transpose_attention(CH + 1)
            x_transpose(0)
            h_transpose(1)
            project_qk(0, 0)
            pe.wait_ge(s_hst, 2)
            project_beta(0, 0)
            transpose_attention(CH + 2)
            project_qk(1, 1)
            transpose_attention(CH + 3)
            x_transpose(1, 1)
            h_product(2)
            transpose_head(0, 0, 0)
            h_transpose(2)
            for h in range(1, HEADS):
                head(0, 0, h)
                if h == 2:
                    h_product(3)
                if h == 5:
                    pe.wait_ge(s_hst, 3)
                    project_beta(1, 1)
                if h == 7:
                    x_transpose(2, 2)
            transpose_head(1, 1, 0)
            project_qk(2, 0)
            gram(0, 0, HEADS - 1)
            for h in range(1, HEADS):
                head(1, 1, h)
                if h == 1:
                    h_transpose(3)
                if h == 4:
                    pe.wait_ge(s_hst, 4)
                    project_beta(2, 0)
                if h == 6:
                    x_transpose(3, 3)
            pe.wait_ge(s_xT, GROUPS)
            with pe.Fori(0, NT // 2 - 2) as m:
                for u in range(2):
                    front(m * 2 + (u + 2), u)
            front(NT - 2, 0)
            transpose_head(NT - 1, 1, 0)
            gram(NT - 2, 0, HEADS - 1)
            for h in range(1, HEADS):
                head(NT - 1, 1, h)
            gram(NT - 1, 1, HEADS - 1)

            def project_values(p, w):
                pe.wait_ge(s_xv[w], (p - w) * 8 + 16)
                for u in range(2):
                    pe.wait_ge(s_vev, p * 2 + u)
                    mm(pgr[:, u, :], xv[:, w, u, :], wqkv[:, 1024:1536], start=True, stop=True).then_inc(s_vp, 1)

            def mix_values(p, w):
                for u in range(2):
                    pe.wait_ge(s_wexp, p * 2 + (u + 1 + 3))
                    pe.wait_ge(s_vev, p * 2 + (u + 1 + 1))
                    pe.wait_ge(s_oTs, p * 2 + (u + 1))
                    for h in range(HEADS):
                        p0 = DH * (h % 2)
                        last = mm(ptr[p0:p0 + DH, u, (h // 2) * P:(h // 2 + 1) * P],
                                  vs[:, w, u, h * DH:(h + 1) * DH], wexp[:, w, u, h, :], start=True, stop=True)
                    last.then_inc(s_oT, 1)
                pe.wait_ge(s_xa, p + 1)
                pe.wait_ge(s_uts, p + 1)
                for u in range(2):
                    pe.wait_ge(s_oTs, p * 2 + (u + 1 + 2))
                    for c in range(4):
                        last = mm(pback[w][:, u * P:(u + 1) * P], oT[:, w, u, c, :], wo[:, c, :], start=(c == 0),
                                  stop=(c == 3))
                    last.then_inc(s_y, 1)

            def first_layer(p, w):
                pe.wait_ge(s_u, p + 2)
                for u in range(2):
                    last = mm(pback[w][0:GIN, (2 + u) * P:(3 + u) * P], U[:, w, u].rearrange("p o k -> p (o k)"),
                              ident_b[:], start=True, stop=True)
                last.then_inc(s_ut, 1)
                pe.wait_ge(s_uts, p + (1 + 2))
                for u in range(2):
                    pe.wait_ge(s_mlp, p * 2 + (u + 1))
                    mm(phid[u][:, 0:3 * HC], UT[:, w, u, :], w1b[:], start=True, stop=True).then_inc(s_hid, 1)

            pe.wait_ge(s_idb, 1)
            pe.wait_ge(s_w1, 1)
            pe.wait_ge(s_xv[0], 16)
            for u in range(2):
                pe.wait_ge(s_comp, 2 + NT - 1 + u)
                mm(pgr[:, u, :], xv[:, 0, u, :], wqkv[:, 1024:1536], start=True, stop=True).then_inc(s_vp, 1)
            mix_values(0, 0)
            project_values(1, 1)
            with pe.Fori(0, PAIRS // 2 - 1) as m:
                for w in range(2):
                    mix_values(m * 2 + (w + 1), 1 - w)
                    project_values(m * 2 + (w + 2), w)
                    first_layer(m * 2 + w, w)
            mix_values(PAIRS - 1, 1)
            first_layer(PAIRS - 2, 0)
            first_layer(PAIRS - 1, 1)


def weight_part():
    return np.concatenate([np.repeat(np.arange(SPLIT), 5), np.tile(np.repeat(np.arange(SPLIT), 3), SPLIT)])


def constants():
    c = np.zeros((P, C_ALL), np.float32)
    p = np.arange(P)
    c[p, C_ID + p] = 1
    c[p, C_M16 + p // STEPS] = 1
    c[p, C_M4 + p % 32 // STEPS] = 1
    t = np.arange(STEPS)
    c[:, C_CAUS:C_CAUS + 64] = (t[None, :] <= t[:, None]).astype(np.float32).reshape(-1)
    for n in range(SPLIT - 1):
        c[0:GIN, C_PART + n] = np.tile(weight_part(), OPS) > n
    c[:, C_RAMP:C_RAMP + 64] = np.tile(16 - np.arange(16), 4)
    c[:, C_IOTA:C_IOTA + 16] = np.arange(16)
    return c


def kernel(**inputs):
    import concourse.bacc as bacc
    from concourse.bass_utils import run_bass_kernel_spmd

    a = {k: np.asarray(v) for k, v in inputs.items()}
    ffn = {op: {n: a[f"L0_ffn_{op}_{n}"] for n in ("w1", "b1", "w2", "b2")} for op in ("and", "or", "xor")}
    wh = a["L0_attn_W_qkvb"].reshape(HEADS, 3 * DH + 1, E)
    wqkv = np.concatenate([np.concatenate([wh[:, DH:2 * DH], wh[:, 0:DH]], 1).reshape(-1, E),
                           wh[:, 2 * DH:3 * DH].reshape(-1, E), wh[:, 3 * DH]], 0).T
    w1 = np.zeros((OPS, 8, 3, HC), np.float32)
    for n, op in enumerate(ffn.values()):
        for r in range(2):
            w1[n, r, r, 0:GE], w1[n, 2 + r, r, 0:GE], w1[n, 4, r, 0:GE] = op["w1"][0], op["w1"][1], op["b1"]
            w1[n, 5, r, 0:GE], w1[n, 6, r, 0:GE], w1[n, 7, r, 0:GE] = op["w1"][46], op["w1"][44], op["w1"][45]
            w1[n, 4, r, GE] = 1
        w1[n, 4, 2, 0:GE], w1[n, 4, 2, GE] = op["w2"][:, 64], op["b2"][64]
    w1 = np.concatenate([np.tile(w1[:, 0:5], (1, SPLIT, 1, 1)), np.tile(w1[:, 5:8], (1, SPLIT * SPLIT, 1, 1))], 1)
    arrays = {
        "spk_rows": a["x"].reshape(-1), "spk_cols": a["x"].T,
        "pre": a["fside_BSS_pre_trace"], "post": a["fside_BSS_post_trace"], "att": a["fside_BSS_attention"],
        "wpre": a["L0_tok_latent_pre_weight"][0], "wpost": a["L0_tok_latent_post_weight"][0],
        "tpre": a["L0_tok_latent_pre_tau_s"][0], "tpost": a["L0_tok_latent_post_tau_s"][0],
        "vwT": a["L0_tok_v_w"].T, "vb": a["L0_tok_v_b"].reshape(E, 1), "wqkvT": wqkv, "woT": a["L0_attn_W_o"].T,
        "lng": a["L0_attn_ln_g"], "lnb": a["L0_attn_ln_b"], "w1": w1.reshape(GIN, 3 * HC),
        "consts": constants(),
    }
    arrays = {k: np.ascontiguousarray(v) for k, v in arrays.items()}
    nc = bacc.Bacc("TRN2", target_bir_lowering=False, num_devices=1)
    args = [nc.dram_tensor(k, v.shape, mybir.dt.from_np(v.dtype), kind="ExternalInput").ap()
            for k, v in arrays.items()]
    out = nc.dram_tensor("out", (STEPS, NEUR, E), F32, kind="ExternalOutput").ap()
    build(nc, *args, out)
    return run_bass_kernel_spmd(nc, [arrays], core_ids=[0]).results[0]["out"]
```
